# Optimizing a Trainium2 kernel written in Bass

```python
import numpy as np
import jax
import jax.numpy as jnp

def _softmax(x, axis=-1):
    return jax.nn.softmax(x, axis=axis)
def _gelu(x):
    return jax.nn.gelu(x, approximate=True)
def _silu(x):
    return jax.nn.silu(x)
def _sigmoid(x):
    return jax.nn.sigmoid(x)
def _layernorm(x, axis=-1, eps=1e-5):
    m = jnp.mean(x, axis=axis, keepdims=True)
    v = jnp.var(x, axis=axis, keepdims=True)
    return (x - m) / jnp.sqrt(v + eps)
def _scatter_add(tgt, idx, src, axis=0):
    return tgt.at[idx].add(src)
def _segment_sum(src, seg, n):
    return jax.ops.segment_sum(src, seg, n)

kernel_name = 'mk_metaformer_d1_conv_nhwc384_1a5eb8'

def setup_inputs(seed: int = 0):
    np.random.seed(seed)
    _w = jnp.asarray
    def _rec_inputs():
        import jax
        import jax.numpy as jnp
        _gk = jax.random.key(seed)
        x = -0.0005963 + 1.001 * jax.random.normal(jax.random.fold_in(_gk, 1), (8, 32, 32, 384), jnp.float32)
        return x
    x = _rec_inputs()
    def _L0_conv_setup():
        import jax, jax.numpy as jnp
        import numpy as np
        B, H, W, DIM = (8, 32, 32, 384)
        HEAD_DIM = 32
        NUM_HEADS = DIM // HEAD_DIM
        ATTN_DIM = NUM_HEADS * HEAD_DIM
        GP_NUM = 20
        key = jax.random.key(seed)
        k1, k2, k3, k4 = jax.random.split(key, 4)
        x = jax.random.normal(k1, (B, H, W, DIM), dtype=jnp.float32)
        W_qkv = jax.random.normal(k2, (DIM, 3 * ATTN_DIM), dtype=jnp.float32) * DIM ** (-0.5)
        gp_w = jax.random.normal(k3, (GP_NUM, DIM), dtype=jnp.float32) * DIM ** (-0.5)
        t_param = jnp.ones((1,), dtype=jnp.float32)
        W_proj = jax.random.normal(k4, (ATTN_DIM, DIM), dtype=jnp.float32) * ATTN_DIM ** (-0.5)
        return {'x': x, 'W_qkv': W_qkv, 'gp_w': gp_w, 't_param': t_param, 'W_proj': W_proj}
    _L0_conv_all = _L0_conv_setup()
    _L0_conv_in = {k: v for k, v in _L0_conv_all.items() if k in ('W_qkv', 'gp_w', 't_param', 'W_proj', )}
    del _L0_conv_all

    def _L0_ffn_setup():
        import jax, jax.numpy as jnp
        import numpy as np
        D_MODEL = 384
        D_FF = 1536
        key = jax.random.key(seed)
        k_x, k1, k2, k3, k4 = jax.random.split(key, 5)
        std = 0.02
        return {'x': jax.random.normal(k_x, (16, 2048, D_MODEL), dtype=jnp.float32), 'c_fc_1': std * jax.random.normal(k1, (1536, 32), dtype=jnp.float32), 'c_fc_2': std * jax.random.normal(k2, (1, 12), dtype=jnp.float32), 'c_proj_1': std * jax.random.normal(k3, (32, 1536), dtype=jnp.float32), 'c_proj_2': std * jax.random.normal(k4, (12, 1), dtype=jnp.float32)}
    _L0_ffn_all = _L0_ffn_setup()
    _L0_ffn_in = {k: v for k, v in _L0_ffn_all.items() if k in ('c_fc_1', 'c_fc_2', 'c_proj_1', 'c_proj_2', )}
    del _L0_ffn_all

    return {
        "x": x,
        "L0_conv_W_qkv": _L0_conv_in["W_qkv"],
        "L0_conv_gp_w": _L0_conv_in["gp_w"],
        "L0_conv_t_param": _L0_conv_in["t_param"],
        "L0_conv_W_proj": _L0_conv_in["W_proj"],
        "L0_ffn_c_fc_1": _L0_ffn_in["c_fc_1"],
        "L0_ffn_c_fc_2": _L0_ffn_in["c_fc_2"],
        "L0_ffn_c_proj_1": _L0_ffn_in["c_proj_1"],
        "L0_ffn_c_proj_2": _L0_ffn_in["c_proj_2"],
    }

def reference(x, L0_conv_W_qkv, L0_conv_gp_w, L0_conv_t_param, L0_conv_W_proj, L0_ffn_c_fc_1, L0_ffn_c_fc_2, L0_ffn_c_proj_1, L0_ffn_c_proj_2):
    import jax
    import jax.numpy as jnp
    def _L0_conv_ref(x, W_qkv, gp_w, t_param, W_proj):
        import jax, jax.numpy as jnp
        import numpy as np
        B, H, W, DIM = (8, 32, 32, 384)
        HEAD_DIM = 32
        NUM_HEADS = DIM // HEAD_DIM
        ATTN_DIM = NUM_HEADS * HEAD_DIM
        GP_NUM = 20
        b, h, w, c = x.shape
        n = h * w
        scale = HEAD_DIM ** (-0.5)
        qkv = x.reshape(b, n, c) @ W_qkv
        q, k, v = jnp.split(qkv, 3, axis=-1)
        q = q.reshape(b, n, NUM_HEADS, HEAD_DIM).transpose(0, 2, 1, 3)
        k = k.reshape(b, n, NUM_HEADS, HEAD_DIM).transpose(0, 2, 1, 3)
        v = v.reshape(b, n, NUM_HEADS, HEAD_DIM).transpose(0, 2, 1, 3)
        attn = jax.nn.softmax(jnp.einsum('bhnd,bhmd->bhnm', q, k) * scale, axis=-1)
        gp = gp_w.reshape(NUM_HEADS, GP_NUM, HEAD_DIM)
        t = jax.nn.softplus(t_param)[0]
        gw = jax.nn.softmax(jnp.einsum('bhnd,hmd->bhnm', q, gp) / t, axis=-1)
        group_weight = jnp.einsum('bhnm,bhkm->bhnk', gw, gw)
        attn = attn * group_weight
        attn = attn / (attn.sum(axis=2, keepdims=True) + 1e-08)
        out = jnp.einsum('bhnm,bhmd->bhnd', attn, v)
        out = out.transpose(0, 2, 1, 3).reshape(b, h, w, ATTN_DIM)
        return out @ W_proj

    def _L0_ffn_ref(x, c_fc_1, c_fc_2, c_proj_1, c_proj_2):
        import jax, jax.numpy as jnp
        import numpy as np
        D_MODEL = 384
        D_FF = 1536
        w_fc = jnp.kron(c_fc_1, c_fc_2)
        w_proj = jnp.kron(c_proj_1, c_proj_2)
        h = x @ w_fc.T
        h = jax.nn.gelu(h, approximate=False)
        out = h @ w_proj.T
        return out

    def _gn(v, G=32, eps=1e-5):
        B_, H_, W_, C_ = v.shape
        g = v.reshape(B_, H_, W_, G, C_ // G)
        m = jnp.mean(g, axis=(1, 2, 4), keepdims=True)
        s = jnp.var(g, axis=(1, 2, 4), keepdims=True)
        return ((g - m) / jnp.sqrt(s + eps)).reshape(v.shape)

    def _ln_c(v, eps=1e-6):
        m = jnp.mean(v, axis=-1, keepdims=True)
        s = jnp.var(v, axis=-1, keepdims=True)
        return (v - m) / jnp.sqrt(s + eps)

    def _ln_t(v, eps=1e-5):
        m = jnp.mean(v, axis=-1, keepdims=True)
        s = jnp.var(v, axis=-1, keepdims=True)
        return (v - m) / jnp.sqrt(s + eps)

    def _to_tokens(v):
        B_, H_, W_, C_ = v.shape
        return v.reshape(B_, H_ * W_, C_)
    def _from_tokens(t, like):
        return t.reshape(like.shape)

    x = x + _L0_conv_ref(_ln_c(x), L0_conv_W_qkv, L0_conv_gp_w, L0_conv_t_param, L0_conv_W_proj)
    t = _to_tokens(x)
    t = t + _L0_ffn_ref(_ln_t(t), L0_ffn_c_fc_1, L0_ffn_c_fc_2, L0_ffn_c_proj_1, L0_ffn_c_proj_2)
    x = _from_tokens(t, x)
    return x


_drawn_inputs = setup_inputs


def setup_inputs(seed=0):
    import zlib

    import numpy as np

    out = dict(_drawn_inputs(seed))
    spreads = {}
    factors = {'L0_conv_gp_w': 8.0,
     'L0_ffn_c_fc_1': 8.0,
     'L0_ffn_c_fc_2': 8.0,
     'L0_ffn_c_proj_1': 8.0,
     'L0_ffn_c_proj_2': 8.0}
    for name, (base, spread) in spreads.items():
        noise = np.random.default_rng([zlib.crc32(name.encode()), seed]).standard_normal(out[name].shape)
        drawn = base * np.exp(spread * noise) if base else spread * noise
        out[name] = jnp.asarray(drawn.astype(out[name].dtype))
    for name, factor in factors.items():
        out[name] = (out[name] * factor).astype(out[name].dtype)
    return out
```

```python
from contextlib import ExitStack

import concourse.bass as bass
from concourse import mybir

F32 = mybir.dt.float32
F32R = mybir.dt.float32r
ALU = mybir.AluOpType
ACT = mybir.ActivationFunctionType
X = mybir.AxisListType.X

P = 128
BATCH, TOK, DIM = 8, 1024, 384
HEAD_DIM, GP_NUM, FF = 32, 20, 1536
HEADS = DIM // HEAD_DIM
HG = P // HEAD_DIM
GROUPS = HEADS // HG
KC = DIM // P
TT = TOK // P
CH = 512
NC = TOK // CH
KRON = 32
KIN = DIM // KRON
FB = FF // P
NT = HG * TT
SCALE = float(HEAD_DIM) ** -0.5
SPLIT = 3 * HEAD_DIM
AUG = SPLIT + 2
PIECES = 3 * HG * 2


def metaformer_layer(nc, x, w_qkv, w_proj, gp_blocks, t_param, fc1, fc2, p1, p2, out):
    x_t = x.rearrange("b (t p) c -> b t p c", p=P)
    out_t = out.rearrange("b (t p) c -> b t p c", p=P)

    with ExitStack() as ctx:
        def sb(name, shape, dt=F32):
            return ctx.enter_context(nc.sbuf_tensor(name, shape, dt))

        def sem(name):
            return ctx.enter_context(nc.semaphore(name))

        wqkv = sb("wqkv", [P, KC, 3 * DIM])
        wproj = sb("wproj", [P, KC, DIM])
        gpb = sb("gpb", [P, GROUPS, HG * GP_NUM])
        fc1_s = sb("fc1_s", [P, FF], F32R)
        fc2_row = sb("fc2_row", [P, DIM])
        p1_s = sb("p1_s", [P, FB, KRON])
        p2_s = sb("p2_s", [P, DIM])
        ident = sb("ident", [P, P])
        tpar = sb("tpar", [P, 8])

        x_in = sb("x_in", [P, 4, DIM])
        xn_t = sb("xn_t", [P, KC, TOK])
        attn_t = sb("attn_t", [P, GROUPS, TOK])
        y = sb("y", [P, 4, DIM])
        yn = sb("yn", [P, 2, DIM])
        z = sb("z", [P, 4, KRON])
        z_hi = sb("z_hi", [KRON, CH], F32R)
        z_lo = sb("z_lo", [KRON, CH], F32R)
        z_s = sb("z_s", [P, CH], F32R)
        stats = sb("stats", [P, 2, 8])
        rstd = sb("rstd", [P, 2, 1])
        var = sb("var", [P, 2, 1])
        minus_half = sb("minus_half", [P, 1])
        mean = sb("mean", [P, 2, 1])

        q_f = sb("q_f", [P, TOK])
        k_f = sb("k_f", [P, TOK])
        hi = [sb(f"hi{i}", [P, TOK], F32R) for i in range(2)]
        lo = [sb(f"lo{i}", [P, TOK], F32R) for i in range(2)]
        v_s = sb("v_s", [P, TT, P])
        q_st = sb("q_st", [AUG, HG, TOK], F32R)
        k_st = sb("k_st", [AUG, HG, TOK], F32R)
        ga_st = sb("ga_st", [SPLIT, HG, TOK], F32R)
        gb_st = sb("gb_st", [SPLIT, HG, TOK], F32R)
        gw = sb("gw", [P, NT, HEAD_DIM])
        gw_f = q_f
        mlp_part = k_f[:, 0:CH]
        gmax = sb("gmax", [P, NT])
        gsum = sb("gsum", [P, NT])
        grec = sb("grec", [P, NT])
        neg_max = sb("neg_max", [P, NT])
        row_sum = sb("row_sum", [P, NT])
        log_sum = sb("log_sum", [P, NT])
        neg_lse = sb("neg_lse", [P, NT])
        lse_hi = sb("lse_hi", [NT, P], F32R)
        lse_lo = sb("lse_lo", [NT, P], F32R)
        attn = sb("attn", [P, 2 * HG, TOK])
        fc1_raw = attn[:, 0:2, :].rearrange("p a n -> p (a n)")[:, 0:FF]
        csum = sb("csum", [P, 2, HG, NC])
        crec = sb("crec", [P, 2, HG])
        vc = sb("vc", [P, 2, HG, HEAD_DIM])

        ps = ctx.enter_context(nc.psum_tensor("ps", [P, 8, CH], F32))

        def wide(slot):
            return ps[:, 2 * slot:2 * slot + 2, :].rearrange("p a n -> p (a n)")

        weights_in, t_in, ident_ok, const_ok = sem("weights_in"), sem("t_in"), sem("ident_ok"), sem("const_ok")
        t_neg, t_exp, t_act, t_dve, fc1_ok = sem("t_neg"), sem("t_exp"), sem("t_act"), sem("t_dve"), sem("fc1_ok")
        x_in_sem = [sem(f"x_loaded{i}") for i in range(4)]
        x_stat, xn_ok, xn_tp, xn_t_ok = sem("x_stat"), sem("xn_ok"), sem("xn_tp"), sem("xn_t_ok")
        q_mm, k_mm, v_mm = sem("q_mm"), sem("k_mm"), sem("v_mm")
        q_ev, k_ev, v_ev = sem("q_ev"), sem("k_ev"), sem("v_ev")
        split_hi, split_ok, stacked = sem("split_hi"), sem("split_ok"), sem("stacked")
        g_mm, g_shift, g_exp, g_rec, g_ok = sem("g_mm"), sem("g_shift"), sem("g_exp"), sem("g_rec"), sem("g_ok")
        g_tp, g_ev, g_split, g_stacked = sem("g_tp"), sem("g_ev"), sem("g_split"), sem("g_stacked")
        s_mm, s_max, s_exp, s_log = sem("s_mm"), sem("s_max"), sem("s_exp"), sem("s_log")
        lse_ok, lse_tp, lse_split, lse_in = sem("lse_ok"), sem("lse_tp"), sem("lse_split"), sem("lse_in")
        st_mm, st_exp, gg_mm, a_ok, c_ok, vc_ok = sem("st_mm"), sem("st_exp"), sem("gg_mm"), sem("a_ok"), sem("c_ok"), sem("vc_ok")
        av_mm, av_ev = sem("av_mm"), sem("av_ev")
        y_in = [sem(f"y_loaded{i}") for i in range(4)]
        pj_mm, y_ok, y_stat, yn_ok, yf_ok, z_ok = sem("pj_mm"), sem("y_ok"), sem("y_stat"), sem("yn_ok"), sem("yf_ok"), sem("z_ok")
        z_tp, zh_ok, zl_ok, z_in = sem("z_tp"), sem("zh_ok"), sem("zl_ok"), sem("z_in")
        h_mm, h_ok, p_mm, p_ev, e_mm, out_ok = sem("h_mm"), sem("h_ok"), sem("p_mm"), sem("p_ev"), sem("e_mm"), sem("out_ok")
        stored = [sem(f"stored{i}") for i in range(4)]
        dve_step, pool_step, rstd_ok = sem("dve_step"), sem("pool_step"), sem("rstd_ok")

        passed = {"sp": sem("sp_passed"), "pool": sem("pool_passed"), "dve": sem("dve_passed")}

        def stand_alone(engine, name):
            engine.sem_inc(passed[name], 1)

        block = ctx.enter_context(nc.Block())

        @block.sync
        def _(sp):
            sp.dma_start(tpar[:, 0:1], t_param).then_inc(t_in, 16)
            for dst, src in ((wqkv[:, :, :], w_qkv), (wproj[:, :, :], w_proj), (gpb[:, :, :], gp_blocks),
                             (fc1_raw[:, :], fc1), (fc2_row[:, :], fc2), (p1_s[:, :, :], p1), (p2_s[:, :], p2)):
                sp.dma_start(dst, src).then_inc(weights_in, 16)

            def stack(pair, dst, signal):
                for j in range(HG):
                    rows = slice(HEAD_DIM * j, HEAD_DIM * (j + 1))
                    for r, part in enumerate(pair):
                        sp.dma_start(dst[HEAD_DIM * r:HEAD_DIM * (r + 1), j, :].bitcast(F32),
                                     part[rows, :].bitcast(F32)).then_inc(signal, 16)

            with sp.Fori(0, BATCH) as b:
                for t in range(TT):
                    sp.wait_ge(xn_tp, b * TT + (t - 3 if t >= 4 else 0))
                    stand_alone(sp, "sp")
                    sp.dma_start(x_in[:, t % 4, :], x_t[b, t]).then_inc(x_in_sem[t % 4], 16)
                for g in range(GROUPS):
                    u = b * GROUPS + g
                    sp.wait_ge(split_ok, u * 2 + 2)
                    stand_alone(sp, "sp")
                    sp.wait_ge(av_mm, u * TT)
                    stack((hi[0], hi[0], lo[0]), q_st, stacked)
                    stack((hi[1], lo[1], hi[1]), k_st, stacked)
                    sp.wait_ge(g_split, u + 1)
                    stack((hi[0], hi[0], lo[0]), ga_st, g_stacked)
                    stack((hi[0], lo[0], hi[0]), gb_st, g_stacked)
                    sp.wait_ge(lse_split, u * 2 + 2)
                    for r, part in enumerate((lse_hi, lse_lo)):
                        sp.dma_start(q_st[SPLIT + r:SPLIT + r + 1, :, :].bitcast(F32).rearrange("o h (t n) -> o (h t) n", n=P),
                                     part[:, :].bitcast(F32)).then_inc(lse_in, 16)
                for c in range(NC):
                    for i in range(4):
                        t = 4 * c + i
                        sp.wait_ge(stored[i], 16 * (b * NC + c))
                        stand_alone(sp, "sp")
                        sp.dma_start(y[:, i, :], x_t[b, t]).then_inc(y_in[i], 16)
                    sp.wait_ge(zh_ok, b * NC + c + 1)
                    sp.wait_ge(zl_ok, b * NC + c + 1)
                    for r, part in enumerate((z_hi, z_lo, z_hi, z_lo)):
                        sp.dma_start(z_s[KRON * r:KRON * (r + 1), :].bitcast(F32), part[:, :].bitcast(F32)).then_inc(z_in, 16)
                    for i in range(4):
                        sp.wait_ge(out_ok, b * TT + 4 * c + i + 1)
                        stand_alone(sp, "sp")
                        sp.dma_start(out_t[b, 4 * c + i], y[:, i, :]).then_inc(stored[i], 16)
            for i in range(4):
                sp.wait_ge(stored[i], 16 * BATCH * NC)

        @block.gpsimd
        def _(pool):
            pool.memset(ident[:, :], 0.0).then_inc(pool_step, 1)
            pool.memset(minus_half[:, :], -0.5).then_inc(pool_step, 1)
            pool.memset(gw[:, :, :], 0.0).then_inc(const_ok, 1)
            pool.wait_ge(pool_step, 2)
            pool.affine_select(out=ident[:, :], in_=ident[:, :], compare_op=ALU.not_equal, fill=1.0, base=0,
                               pattern=[[-1, P]], channel_multiplier=1).then_inc(ident_ok, 1)
            pool.wait_ge(weights_in, 16 * 7)
            pool.tensor_copy(fc1_s[:, :], fc1_raw[:, :]).then_inc(fc1_ok, 1)
            pool.wait_ge(fc1_ok, 1)
            pool.tensor_tensor(fc1_s[64:P, :], fc1_raw[64:P, :], fc1_s[64:P, :].bitcast(F32),
                               ALU.subtract).then_inc(fc1_ok, 1)
            pool.wait_ge(fc1_ok, 2)

            with pool.Fori(0, BATCH) as b:
                for t in range(TT):
                    pool.wait_ge(x_stat, b * TT + t + 1)
                    pool.tensor_tensor(rstd[:, t % 2, :], var[:, t % 2, :], minus_half[:, :],
                                       ALU.pow).then_inc(rstd_ok, 1)
                    pool.wait_ge(rstd_ok, b * 2 * TT + t + 1)
                    stand_alone(pool, "pool")
                    pool.tensor_scalar(x_in[:, t % 4, :], x_in[:, t % 4, :], mean[:, t % 2, :], rstd[:, t % 2, :],
                                       ALU.subtract, ALU.mult).then_inc(xn_ok, 1)
                for g in range(GROUPS):
                    u = b * GROUPS + g
                    for i, (src, ready) in enumerate(((q_f, q_ev), (k_f, k_ev))):
                        pool.wait_ge(ready, u + 1)
                        pool.wait_ge(stacked, u * PIECES * 16)
                        pool.wait_ge(g_stacked, u * PIECES * 16)
                        stand_alone(pool, "pool")
                        pool.tensor_copy(hi[i][:, :], src[:, :]).then_inc(split_hi, 1)
                        pool.wait_ge(split_hi, u * 3 + i + 1)
                        pool.tensor_tensor(lo[i][:, :], src[:, :], hi[i][:, :].bitcast(F32),
                                           ALU.subtract).then_inc(split_ok, 1)
                    pool.wait_ge(g_rec, u + 1)
                    pool.tensor_tensor(gw[:, :, 0:GP_NUM], gw[:, :, 0:GP_NUM],
                                       grec[:, :].unsqueeze(2).broadcast_to([P, NT, GP_NUM]),
                                       ALU.mult).then_inc(g_ok, 1)
                    pool.wait_ge(g_ev, u + 1)
                    pool.wait_ge(stacked, (u + 1) * PIECES * 16)
                    stand_alone(pool, "pool")
                    pool.tensor_copy(hi[0][:, :], gw_f[:, :]).then_inc(split_hi, 1)
                    pool.wait_ge(split_hi, u * 3 + 3)
                    pool.tensor_tensor(lo[0][:, :], gw_f[:, :], hi[0][:, :].bitcast(F32),
                                       ALU.subtract).then_inc(g_split, 1)
                    for m in range(TT):
                        pool.wait_ge(c_ok, u * TT + m + 1)
                        pool.wait_ge(v_ev, u + 1)
                        if m >= 2:
                            pool.wait_ge(av_mm, u * TT + m - 1)
                        pool.tensor_tensor(vc[:, m % 2, :, :],
                                           v_s[:, m, :].rearrange("p (h d) -> p h d", h=HG),
                                           crec[:, m % 2, :].unsqueeze(2).broadcast_to([P, HG, HEAD_DIM]),
                                           ALU.mult).then_inc(vc_ok, 1)
                for t in range(TT):
                    pool.wait_ge(y_stat, b * TT + t + 1)
                    if t >= 2:
                        pool.wait_ge(z_ok, b * TT + t - 1)
                    pool.tensor_tensor(rstd[:, t % 2, :], var[:, t % 2, :], minus_half[:, :],
                                       ALU.pow).then_inc(rstd_ok, 1)
                    pool.wait_ge(rstd_ok, (2 * b + 1) * TT + t + 1)
                    stand_alone(pool, "pool")
                    pool.tensor_scalar(yn[:, t % 2, :], y[:, t % 4, :], mean[:, t % 2, :], rstd[:, t % 2, :],
                                       ALU.subtract, ALU.mult).then_inc(yn_ok, 1)
                    pool.wait_ge(yn_ok, b * TT + t + 1)
                    pool.tensor_tensor(yn[:, t % 2, :], yn[:, t % 2, :], fc2_row[:, :], ALU.mult).then_inc(yf_ok, 1)

        @block.scalar
        def _(act):
            act.wait_ge(t_dve, 1)
            act.activation(tpar[:, 2:3], tpar[:, 1:2], ACT.Exp).then_inc(t_exp, 1)
            act.wait_ge(t_exp, 1)
            act.activation(tpar[:, 3:4], tpar[:, 2:3], ACT.Ln, bias=1.0).then_inc(t_act, 1)

            with act.Fori(0, BATCH) as b:
                for t in range(TT):
                    act.wait_ge(xn_tp, b * TT + t + 1)
                    act.copy(xn_t[:, :, t * P:(t + 1) * P],
                             ps[:, t, 0:DIM].rearrange("p (k n) -> p k n", k=KC)).then_inc(xn_t_ok, 1)
                for g in range(GROUPS):
                    u = b * GROUPS + g
                    act.wait_ge(q_mm, u + 1)
                    act.wait_ge(g_split, u)
                    act.mul(q_f[:, :], wide(0), SCALE).then_inc(q_ev, 1)
                    act.wait_ge(k_mm, u + 1)
                    act.copy(k_f[:, :], wide(1)).then_inc(k_ev, 1)
                    act.wait_ge(v_mm, u + 1)
                    act.wait_ge(vc_ok, u * TT)
                    act.copy(v_s[:, :, :].rearrange("p t n -> p (t n)"), wide(2)).then_inc(v_ev, 1)
                    act.wait_ge(g_shift, u * 2 + 2)
                    act.wait_ge(t_dve, 4)
                    act.activation(gw[:, :, 0:GP_NUM], gw[:, :, 0:GP_NUM], ACT.Exp,
                                   scale=tpar[:, 6:7]).then_inc(g_exp, 1)
                    act.wait_ge(g_tp, u + 1)
                    act.wait_ge(split_ok, u * 2 + 2)
                    act.copy(gw_f[:, :], wide(0)).then_inc(g_ev, 1)
                    for i in range(NT):
                        act.wait_ge(s_max, u * NT + i + 1)
                        act.activation(wide(i % 4), wide(i % 4), ACT.Exp, bias=neg_max[:, i:i + 1],
                                       accum_out=row_sum[:, i:i + 1]).then_inc(s_exp, 1)
                    act.wait_ge(s_exp, (u + 1) * NT)
                    act.activation(log_sum[:, :], row_sum[:, :], ACT.Ln).then_inc(s_log, 1)
                    for i in range(NT):
                        act.wait_ge(st_mm, u * NT + i + 1)
                        if i >= 2 * HG:
                            act.wait_ge(av_mm, u * TT + i // HG - 1)
                        act.activation(attn[:, i % (2 * HG), :], wide(i % 2), ACT.Exp).then_inc(st_exp, 1)
                    act.wait_ge(av_mm, (u + 1) * TT)
                    act.copy(attn_t[:, g, :], wide(3)).then_inc(av_ev, 1)
                for c in range(NC):
                    bc = b * NC + c
                    act.wait_ge(z_tp, bc + 1)
                    act.wait_ge(z_in, 64 * bc)
                    act.copy(z_hi[:, :], ps[0:KRON, 4, :]).then_inc(zh_ok, 1)
                    for f in range(FB):
                        act.wait_ge(h_mm, bc * FB + f + 1)
                        if f >= 2 * HG:
                            act.wait_ge(p_mm, bc * KC + f // 4 - 1)
                        act.activation(attn[:, f % (2 * HG), 0:CH], ps[:, 5 + f % 2, :], ACT.Gelu).then_inc(h_ok, 1)
                    act.wait_ge(p_mm, (bc + 1) * KC)
                    act.copy(mlp_part[:, :], ps[:, 7, :]).then_inc(p_ev, 1)

        @block.tensor
        def _(pe):
            pe.wait_ge(ident_ok, 1)
            pe.wait_ge(const_ok, 2)
            pe.wait_ge(weights_in, 16 * 7)
            pe.wait_ge(fc1_ok, 2)
            with pe.Fori(0, BATCH) as b:
                pe.wait_ge(out_ok, b * TT)
                for t in range(TT):
                    pe.wait_ge(xn_ok, b * TT + t + 1)
                    for k in range(KC):
                        mm = pe.transpose(ps[:, t, k * P:(k + 1) * P], x_in[:, t % 4, k * P:(k + 1) * P], ident[:, :])
                    mm.then_inc(xn_tp, 1)
                pe.wait_ge(xn_t_ok, b * TT + TT)
                for g in range(GROUPS):
                    u = b * GROUPS + g
                    pe.wait_ge(av_ev, u)
                    for part, done in ((0, q_mm), (1, k_mm)):
                        cols = slice(part * DIM + g * P, part * DIM + (g + 1) * P)
                        for c in range(NC):
                            for k in range(KC):
                                mm = pe.matmul(ps[:, 2 * part + c, :], wqkv[:, k, cols],
                                               xn_t[:, k, c * CH:(c + 1) * CH], start=(k == 0), stop=(k == KC - 1))
                        mm.then_inc(done, 1)
                    for t in range(TT):
                        for k in range(KC):
                            mm = pe.matmul(ps[:, 4 + t // 4, (t % 4) * P:(t % 4 + 1) * P],
                                           xn_t[:, k, t * P:(t + 1) * P],
                                           wqkv[:, k, 2 * DIM + g * P:2 * DIM + (g + 1) * P],
                                           start=(k == 0), stop=(k == KC - 1))
                    mm.then_inc(v_mm, 1)
                    pe.wait_ge(q_ev, u + 1)
                    w = HG * GP_NUM
                    for t in range(TT):
                        mm = pe.matmul(ps[:, 6 + t // 4, (t % 4) * w:(t % 4 + 1) * w], q_f[:, t * P:(t + 1) * P],
                                       gpb[:, g, :], start=True, stop=True)
                    mm.then_inc(g_mm, 1)
                    pe.wait_ge(g_ok, u + 1)
                    for t in range(TT):
                        mm = pe.transpose(ps[:, t // 4, (t % 4) * P:(t % 4 + 1) * P],
                                          gw[:, HG * t:HG * (t + 1), :].rearrange("p h m -> p (h m)"), ident[:, :])
                    mm.then_inc(g_tp, 1)
                    pe.wait_ge(stacked, (u + 1) * PIECES * 16)
                    pe.wait_ge(g_ev, u + 1)
                    pe.wait_ge(k_ev, u + 1)
                    pe.wait_ge(v_ev, u + 1)
                    for i in range(NT):
                        h, t = i // TT, i % TT
                        if i >= 4:
                            pe.wait_ge(s_exp, u * NT + i - 3)
                        for c in range(NC):
                            mm = pe.matmul(ps[:, 2 * (i % 4) + c, :], q_st[0:SPLIT, h, t * P:(t + 1) * P],
                                           k_st[0:SPLIT, h, c * CH:(c + 1) * CH], start=True, stop=True)
                        mm.then_inc(s_mm, 1)
                    pe.wait_ge(lse_ok, u + 1)
                    pe.transpose(ps[0:NT, 0, 0:P], neg_lse[:, :], ident[:, :]).then_inc(lse_tp, 1)
                    pe.wait_ge(lse_in, (u + 1) * 32)
                    pe.wait_ge(g_stacked, (u + 1) * PIECES * 16)

                    def weigh_values(m):
                        pe.wait_ge(vc_ok, u * TT + m + 1)
                        for c in range(NC):
                            for h in range(HG):
                                mm = pe.matmul(ps[HEAD_DIM * h:HEAD_DIM * (h + 1), 6 + c, :], vc[:, m % 2, h, :],
                                               attn[:, HG * (m % 2) + h, c * CH:(c + 1) * CH],
                                               start=(m == 0), stop=(m == TT - 1))
                        mm.then_inc(av_mm, 1)

                    for i in range(NT):
                        m, h = i // HG, i % HG
                        if i >= 2:
                            pe.wait_ge(st_exp, u * NT + i - 1)
                        for c in range(NC):
                            mm = pe.matmul(ps[:, 2 * (i % 2) + c, :], k_st[:, h, m * P:(m + 1) * P],
                                           q_st[:, h, c * CH:(c + 1) * CH], start=True, stop=True)
                        mm.then_inc(st_mm, 1)
                        for c in range(NC):
                            if i >= 1:
                                pe.wait_ge(a_ok, u * 2 * NT + 2 * (i - 1) + c + 1)
                            pe.matmul(ps[:, 4 + c, :], ga_st[:, h, m * P:(m + 1) * P],
                                      gb_st[:, h, c * CH:(c + 1) * CH], start=True, stop=True).then_inc(gg_mm, 1)
                        if h == HG - 1 and m > 0:
                            weigh_values(m - 1)
                    weigh_values(TT - 1)
                pe.wait_ge(av_ev, (b + 1) * GROUPS)
                for c in range(NC):
                    bc = b * NC + c
                    pe.wait_ge(out_ok, bc * 4)
                    for i in range(4):
                        t = 4 * c + i
                        for k in range(KC):
                            mm = pe.matmul(ps[:, i, 0:DIM], attn_t[:, k, t * P:(t + 1) * P], wproj[:, k, :],
                                           start=(k == 0), stop=(k == KC - 1))
                        mm.then_inc(pj_mm, 1)
                    for i in range(4):
                        pe.wait_ge(z_ok, b * TT + 4 * c + i + 1)
                        mm = pe.transpose(ps[0:KRON, 4, i * P:(i + 1) * P], z[:, i, :], ident[:, :])
                    mm.then_inc(z_tp, 1)
                    pe.wait_ge(z_in, 64 * (bc + 1))

                    def mlp_out(r):
                        pe.wait_ge(h_ok, bc * FB + 4 * r + 4)
                        for j in range(4):
                            f = 4 * r + j
                            mm = pe.matmul(ps[KRON * j:KRON * (j + 1), 7, :], p1_s[:, f, :],
                                           attn[:, f % (2 * HG), 0:CH], start=(r == 0), stop=(r == FB // 4 - 1))
                        mm.then_inc(p_mm, 1)

                    for f in range(FB):
                        if f >= 2:
                            pe.wait_ge(h_ok, bc * FB + f - 1)
                        pe.matmul(ps[:, 5 + f % 2, :], fc1_s[:, f * P:(f + 1) * P], z_s[:, :],
                                  start=True, stop=True).then_inc(h_mm, 1)
                        if f % 4 == 1 and f > 4:
                            mlp_out(f // 4 - 1)
                    mlp_out(FB // 4 - 1)
                    pe.wait_ge(p_ev, bc + 1)
                    pe.wait_ge(y_ok, b * TT + 4 * c + 4)
                    for i in range(4):
                        pe.matmul(ps[:, i, 0:DIM], mlp_part[:, i * P:(i + 1) * P], p2_s[:, :],
                                  start=True, stop=True).then_inc(e_mm, 1)

        @block.vector
        def _(dve):
            dve.memset(k_st[SPLIT:AUG, :, :].bitcast(F32), 1.0).then_inc(const_ok, 1)
            dve.wait_ge(t_in, 16)
            dve.tensor_scalar(tpar[:, 7:8], tpar[:, 0:1], -1.0, None, ALU.mult).then_inc(t_neg, 1)
            dve.wait_ge(t_neg, 1)
            dve.tensor_tensor(tpar[:, 1:2], tpar[:, 0:1], tpar[:, 7:8], ALU.min).then_inc(t_dve, 1)
            dve.wait_ge(t_act, 1)
            dve.scalar_tensor_tensor(tpar[:, 4:5], tpar[:, 0:1], 0.0, tpar[:, 3:4], ALU.max, ALU.add).then_inc(t_dve, 1)
            dve.wait_ge(t_dve, 2)
            dve.tensor_scalar(tpar[:, 5:6], tpar[:, 4:5], SCALE, None, ALU.mult).then_inc(t_dve, 1)
            dve.wait_ge(t_dve, 3)
            dve.reciprocal(tpar[:, 6:7], tpar[:, 5:6]).then_inc(t_dve, 1)

            per_batch = 2 * TT * 3 + GROUPS * (3 + TT)

            with dve.Fori(0, BATCH) as b:
                steps = [0]

                def step(ins):
                    steps[0] += 1
                    ins.then_inc(dve_step, 1)
                    dve.wait_ge(dve_step, b * per_batch + steps[0])

                def layer_stats(src, t, eps, signal):
                    step(dve.bn_stats(stats[:, t % 2, 0:6], src))
                    stand_alone(dve, "dve")
                    step(dve.bn_aggr(stats[:, t % 2, 6:8], stats[:, t % 2, 0:6]))
                    step(dve.tensor_copy(mean[:, t % 2, :], stats[:, t % 2, 6:7]))
                    dve.tensor_scalar(var[:, t % 2, :], stats[:, t % 2, 7:8], eps, None, ALU.add).then_inc(signal, 1)

                for t in range(TT):
                    dve.wait_ge(x_in_sem[t % 4], 16 * (2 * b + t // 4 + 1))
                    if t >= 2:
                        dve.wait_ge(xn_ok, b * TT + t - 1)
                    layer_stats(x_in[:, t % 4, :], t, 1e-6, x_stat)
                for g in range(GROUPS):
                    u = b * GROUPS + g
                    dve.wait_ge(g_mm, u + 1)
                    dve.wait_ge(g_tp, u)
                    n = NT // 2
                    for i in range(2):
                        logits = ps[:, 6 + i, 0:n * GP_NUM].rearrange("p (a m) -> p a m", m=GP_NUM)
                        step(dve.tensor_reduce(gmax[:, n * i:n * (i + 1)], logits, X, ALU.max))
                        dve.tensor_tensor(gw[:, n * i:n * (i + 1), 0:GP_NUM], logits,
                                          gmax[:, n * i:n * (i + 1)].unsqueeze(2).broadcast_to([P, n, GP_NUM]),
                                          ALU.subtract).then_inc(g_shift, 1)
                    dve.wait_ge(g_exp, u + 1)
                    step(dve.tensor_reduce(gsum[:, :], gw[:, :, 0:GP_NUM], X, ALU.add))
                    dve.reciprocal(grec[:, :], gsum[:, :]).then_inc(g_rec, 1)
                    for i in range(NT):
                        dve.wait_ge(s_mm, u * NT + i + 1)
                        dve.tensor_reduce(neg_max[:, i:i + 1], wide(i % 4), X, ALU.max,
                                          negate=True).then_inc(s_max, 1)
                    dve.wait_ge(s_log, u + 1)
                    dve.tensor_tensor(neg_lse[:, :], neg_max[:, :], log_sum[:, :], ALU.subtract).then_inc(lse_ok, 1)
                    dve.wait_ge(lse_tp, u + 1)
                    dve.tensor_copy(lse_hi[:, :], ps[0:NT, 0, 0:P]).then_inc(lse_split, 1)
                    dve.wait_ge(lse_split, u * 2 + 1)
                    dve.tensor_tensor(lse_lo[:, :], ps[0:NT, 0, 0:P], lse_hi[:, :].bitcast(F32),
                                      ALU.subtract).then_inc(lse_split, 1)
                    for i in range(NT):
                        m, h = i // HG, i % HG
                        dve.wait_ge(st_exp, u * NT + i + 1)
                        for c in range(NC):
                            dve.wait_ge(gg_mm, u * 2 * NT + 2 * i + c + 1)
                            a = attn[:, i % (2 * HG), c * CH:(c + 1) * CH]
                            dve.tensor_tensor_reduce(a, ps[:, 4 + c, :], a, 1.0, 0.0, ALU.mult, ALU.add,
                                                     csum[:, m % 2, h, c:c + 1]).then_inc(a_ok, 1)
                        if h == HG - 1:
                            dve.wait_ge(a_ok, (u * NT + i + 1) * 2)
                            if m >= 2:
                                dve.wait_ge(vc_ok, u * TT + m - 1)
                            step(dve.scalar_tensor_tensor(crec[:, m % 2, :], csum[:, m % 2, :, 0], 1e-8,
                                                          csum[:, m % 2, :, 1], ALU.add, ALU.add))
                            dve.reciprocal(crec[:, m % 2, :], crec[:, m % 2, :]).then_inc(c_ok, 1)


                for c in range(NC):
                    bc = b * NC + c
                    for i in range(4):
                        t = 4 * c + i
                        dve.wait_ge(y_in[i], 16 * (bc + 1))
                        dve.wait_ge(pj_mm, b * TT + t + 1)
                        dve.tensor_tensor(y[:, i, :], ps[:, i, 0:DIM], y[:, i, :], ALU.add).then_inc(y_ok, 1)
                        dve.wait_ge(y_ok, b * TT + t + 1)
                        if t >= 2:
                            dve.wait_ge(yn_ok, b * TT + t - 1)
                        layer_stats(y[:, i, :], t, 1e-5, y_stat)
                        dve.wait_ge(yf_ok, b * TT + t + 1)
                        dve.tensor_reduce(z[:, i, :], yn[:, t % 2, :].rearrange("p (j l) -> p j l", l=KIN),
                                          X, ALU.add).then_inc(z_ok, 1)
                    dve.wait_ge(zh_ok, bc + 1)
                    dve.tensor_tensor(z_lo[:, :], ps[0:KRON, 4, :], z_hi[:, :].bitcast(F32),
                                      ALU.subtract).then_inc(zl_ok, 1)
                    for i in range(4):
                        dve.wait_ge(e_mm, b * TT + 4 * c + i + 1)
                        dve.tensor_tensor(y[:, i, :], ps[:, i, 0:DIM], y[:, i, :], ALU.add).then_inc(out_ok, 1)
                assert steps[0] == per_batch, steps


def kernel(x, L0_conv_W_qkv, L0_conv_gp_w, L0_conv_t_param, L0_conv_W_proj,
           L0_ffn_c_fc_1, L0_ffn_c_fc_2, L0_ffn_c_proj_1, L0_ffn_c_proj_2):
    import numpy as np
    import concourse.bacc as bacc
    from concourse.bass_utils import run_bass_kernel_spmd

    def rows(w):
        w = np.asarray(w)
        return np.ascontiguousarray(w.reshape(-1, P, w.shape[1]).transpose(1, 0, 2))

    gp = np.asarray(L0_conv_gp_w).reshape(GROUPS, HG, GP_NUM, HEAD_DIM)
    blocks = np.zeros((HG, HEAD_DIM, GROUPS, HG, GP_NUM), gp.dtype)
    for j in range(HG):
        blocks[j, :, :, j, :] = gp[:, j].transpose(2, 0, 1)
    spread = np.zeros((4, KRON, KRON, KIN), np.asarray(L0_ffn_c_proj_2).dtype)
    for j in range(KRON):
        spread[:, j, j, :] = np.asarray(L0_ffn_c_proj_2)[:, 0]
    arrays = {
        "x": np.ascontiguousarray(np.asarray(x).reshape(BATCH, TOK, DIM)),
        "w_qkv": rows(L0_conv_W_qkv),
        "w_proj": rows(L0_conv_W_proj),
        "gp_blocks": blocks.reshape(P, GROUPS, HG * GP_NUM),
        "t_param": np.ascontiguousarray(np.broadcast_to(np.asarray(L0_conv_t_param).reshape(1, 1), (P, 1))),
        "fc1": np.ascontiguousarray(np.tile(np.asarray(L0_ffn_c_fc_1).T, (4, 1))),
        "fc2": np.ascontiguousarray(np.broadcast_to(np.tile(np.asarray(L0_ffn_c_fc_2)[0], KRON), (P, DIM))),
        "p1": np.ascontiguousarray(np.asarray(L0_ffn_c_proj_1).reshape(KRON, FB, P).transpose(2, 1, 0)),
        "p2": spread.reshape(P, DIM),
    }
    nc = bacc.Bacc("TRN2", target_bir_lowering=False, num_devices=1)
    args = [nc.dram_tensor(name, a.shape, mybir.dt.from_np(a.dtype), kind="ExternalInput").ap()
            for name, a in arrays.items()]
    args.append(nc.dram_tensor("out", (BATCH, TOK, DIM), F32, kind="ExternalOutput").ap())
    metaformer_layer(nc, *args)
    r = run_bass_kernel_spmd(nc, [arrays], core_ids=[0])
    return r.results[0]["out"].reshape(np.asarray(x).shape)
```

```python
from contextlib import ExitStack

import concourse.bass as bass
from concourse import mybir

F32 = mybir.dt.float32
F32R = mybir.dt.float32r
ALU = mybir.AluOpType
ACT = mybir.ActivationFunctionType
X = mybir.AxisListType.X

P = 128
BATCH, TOK, DIM = 8, 1024, 384
HEAD_DIM, GP_NUM, FF = 32, 20, 1536
HEADS = DIM // HEAD_DIM
HG = P // HEAD_DIM
GROUPS = HEADS // HG
KC = DIM // P
TT = TOK // P
CH = 512
NC = TOK // CH
KRON = 32
KIN = DIM // KRON
FB = FF // P
NT = HG * TT
SCALE = float(HEAD_DIM) ** -0.5
SPLIT = 3 * HEAD_DIM
AUG = SPLIT + 2


def metaformer_layer(nc, x, w_qkv, w_proj, gp_blocks, t_param, fc1, fc2, p1, p2, out):
    x_t = x.rearrange("b (t p) c -> b t p c", p=P)
    out_t = out.rearrange("b (t p) c -> b t p c", p=P)

    with ExitStack() as ctx:
        def sb(name, shape, dt=F32):
            return ctx.enter_context(nc.sbuf_tensor(name, shape, dt))

        def sem(name):
            return ctx.enter_context(nc.semaphore(name))

        wqkv = sb("wqkv", [P, KC, 3 * DIM])
        wproj = sb("wproj", [P, KC, DIM])
        gpb = sb("gpb", [P, GROUPS, HG * GP_NUM])
        fc1_s = sb("fc1_s", [P, FF], F32R)
        fc2_row = sb("fc2_row", [P, DIM])
        p1_s = sb("p1_s", [P, FB, KRON])
        p2_s = sb("p2_s", [P, DIM])
        ident = sb("ident", [P, P])
        tpar = sb("tpar", [P, 8])

        x_in = sb("x_in", [P, 4, DIM])
        xn_t = sb("xn_t", [P, KC, TOK])
        attn_t = sb("attn_t", [P, GROUPS, TOK])
        y = sb("y", [P, 4, DIM])
        z = sb("z", [P, 4, KRON])
        z_s = sb("z_s", [P, CH], F32R)
        x_stats_s = sb("x_stats_s", [P, TT, 8])
        x_var = sb("x_var", [P, TT])
        x_rstd = sb("x_rstd", [P, TT])
        y_stats_s = sb("y_stats_s", [P, 4, 8])
        y_var = sb("y_var", [P, 4])
        y_rstd = sb("y_rstd", [P, 4])
        minus_half = sb("minus_half", [P, 4])
        eps1 = sb("eps1", [P, 1])
        eps2 = sb("eps2", [P, 4])

        src = sb("src", [P, TOK])
        hi = [sb(f"{n}_hi", [P, TOK], F32R) for n in ("q", "k", "g")]
        lo = [sb(f"{n}_lo", [P, TOK], F32R) for n in ("q", "k", "g")]
        gw = sb("gw", [P, NT, HEAD_DIM])
        gmax = sb("gmax", [P, NT])
        gsum = sb("gsum", [P, NT])
        grec = sb("grec", [P, NT])
        v_s = sb("v_s", [P, TOK])
        q_st = sb("q_st", [AUG, HG, TOK], F32R)
        k_st = sb("k_st", [AUG, HG, TOK], F32R)
        ga_st = sb("ga_st", [SPLIT, HG, TOK], F32R)
        gb_st = sb("gb_st", [SPLIT, HG, TOK], F32R)
        neg_max = sb("neg_max", [P, NT])
        row_sum = sb("row_sum", [P, NT])
        log_sum = sb("log_sum", [P, NT])
        neg_lse = sb("neg_lse", [P, NT])
        lse_hi = sb("lse_hi", [TT, P], F32R)
        lse_lo = sb("lse_lo", [TT, P], F32R)
        attn = sb("attn", [P, 2 * HG, TOK])
        csum = sb("csum", [P, 2, HG, NC])
        crec = sb("crec", [P, 2, HG])
        vc = sb("vc", [P, 2, HG, HEAD_DIM])
        fc1_raw = attn[:, 4:6, :].rearrange("p a n -> p (a n)")[:, 0:FF]
        x_late = attn[:, 0:4, 0:DIM]
        k_src = attn[:, 2 * HG - 1, :]
        yn = attn[:, 0:4, CH:CH + DIM]
        mlp_part = attn[:, 6, CH:2 * CH]

        ps = ctx.enter_context(nc.psum_tensor("ps", [P, 8, CH], F32))

        def wide(slot):
            return ps[:, 2 * slot:2 * slot + 2, :].rearrange("p a n -> p (a n)")

        weights_in, t_in, ident_ok, const_ok = sem("weights_in"), sem("t_in"), sem("ident_ok"), sem("const_ok")
        t_neg, t_exp, t_act, t_dve, fc1_ok = sem("t_neg"), sem("t_exp"), sem("t_act"), sem("t_dve"), sem("fc1_ok")
        x_loaded = [sem("x_loaded0"), sem("x_loaded1")]
        x_stat, x_var_ok, x_rstd_ok, xn_ok = sem("x_stat"), sem("x_var_ok"), sem("x_rstd_ok"), sem("xn_ok")
        side_mm = [sem("side_mm0"), sem("side_mm1")]
        side_free = [sem("side_free0"), sem("side_free1")]
        split_hi, q_split, k_split, g_split = sem("split_hi"), sem("q_split"), sem("k_split"), sem("g_split")
        stacked = [sem(f"stacked{h}") for h in range(HG)]
        g_exp, g_rec, g_ok, g_stacked = sem("g_exp"), sem("g_rec"), sem("g_ok"), sem("g_stacked")
        s_mm, s_max, s_exp, s_log = sem("s_mm"), sem("s_max"), sem("s_exp"), sem("s_log")
        lse_ok, lse_hi_ok = sem("lse_ok"), sem("lse_hi_ok")
        lse_in = [sem(f"lse_in{h}") for h in range(HG)]
        st_mm, st_exp, gg_mm, a_ok, c_ok, vc_ok = sem("st_mm"), sem("st_exp"), sem("gg_mm"), sem("a_ok"), sem("c_ok"), sem("vc_ok")
        av_mm, av_ev = sem("av_mm"), sem("av_ev")
        y_in = [sem("y_loaded0"), sem("y_loaded1")]
        pj_mm, y_ok, y_stat, y_var_ok, y_rstd_ok, z_ok = sem("pj_mm"), sem("y_ok"), sem("y_stat"), sem("y_var_ok"), sem("y_rstd_ok"), sem("z_ok")
        z_tp, zh_ok, zl_ok = sem("z_tp"), sem("zh_ok"), sem("zl_ok")
        h_mm, h_ok, p_mm, p_ev, e_mm, out_ok = sem("h_mm"), sem("h_ok"), sem("p_mm"), sem("p_ev"), sem("e_mm"), sem("out_ok")
        stored = [sem("stored0"), sem("stored1")]
        dve_step, pool_step = sem("dve_step"), sem("pool_step")
        passed = {"sp": sem("sp_passed"), "pool": sem("pool_passed"), "dve": sem("dve_passed")}

        def stand_alone(engine, name):
            engine.sem_inc(passed[name], 1)

        def side_work(g, more):
            if g < GROUPS - 1:
                return [(0, "g", 0, 1), (1, "g", 1, 1), (2, "v", 0, 4), (6, "v", 1, 4), (10, "q", 0, 3),
                        (13, "q", 1, 3), (14, "lse", 0, 1), (17, "logit", 0, 1), (18, "logit", 1, 1),
                        (19, "k", 0, 3), (22, "lse", 1, 1), (23, "k", 1, 3), (30, "lse", 2, 1), (NT, "lse", 3, 1)]
            if more:
                return ([(0, "g", 0, 1), (1, "g", 1, 1), (2, "v", 0, 2), (4, "v", 1, 2), (5, "x", 0, 1)] +
                        [(6 + t, "x", t, 1) for t in range(1, TT)] +
                        [(14, "lse", 0, 1), (15, "q", 0, 2), (17, "q", 1, 2), (20, "logit", 0, 1),
                         (21, "logit", 1, 1), (22, "lse", 1, 1), (23, "k", 0, 3), (26, "k", 1, 3),
                         (30, "lse", 2, 1), (NT, "lse", 3, 1)])
            return [(0, "g", 0, 1), (1, "g", 1, 1), (2, "v", 0, 4), (6, "v", 1, 4), (14, "lse", 0, 1),
                    (22, "lse", 1, 1), (30, "lse", 2, 1), (NT, "lse", 3, 1)]

        FIRST = [(0, "x", t, 1) for t in range(TT)] + [(0, w, i, 1) for w in ("q", "logit", "k") for i in range(2)]
        PER_BATCH = [len(side_work(g, True)) for g in range(GROUPS)]
        BEFORE = [sum(PER_BATCH[:g]) for g in range(GROUPS)]

        def side_count(b, g, n):
            if b is None:
                return n // 2
            return len(FIRST) // 2 + b * (sum(PER_BATCH) // 2) + (BEFORE[g] + n) // 2

        def side_bank(b, g, n):
            return n % 2 if b is None else (BEFORE[g] + n) % 2

        def wait_side(engine, signal, b, g, more, what, part):
            work = FIRST if b is None else side_work(g, more)
            n = [w[1:3] for w in work].index((what, part))
            engine.wait_ge(signal[side_bank(b, g, n)], side_count(b, g, n) + 1)

        def run(engine, side, scores, products, post):
            for n, (_, what, part, _) in enumerate(FIRST):
                side(None, 0, True, n, what, part, 0)

            def batch(b, more):
                for g in range(GROUPS):
                    scores(b, g, more)
                    products(b, g, more)
                post(b, more)

            with engine.Fori(0, BATCH - 1) as b:
                batch(b, True)
            batch(BATCH - 1, False)

        def between(lag, i, side, b, g, more, u):
            for n, (at, what, part, length) in enumerate(side_work(g, more)):
                due = min(max(at + length - 1 + lag(what), 0), NT - 1) if at < NT else NT
                if due == i:
                    side(b, g, more, n, what, part, u + 1)

        block = ctx.enter_context(nc.Block())

        @block.sync
        def _(sp):
            sp.dma_start(tpar[:, 0:1], t_param).then_inc(t_in, 16)
            for dst, src_ in ((wqkv[:, :, :], w_qkv), (wproj[:, :, :], w_proj), (gpb[:, :, :], gp_blocks),
                              (fc1_raw[:, :], fc1), (fc2_row[:, :], fc2), (p1_s[:, :, :], p1), (p2_s[:, :], p2)):
                sp.dma_start(dst, src_).then_inc(weights_in, 16)
            for c in range(NC):
                sp.sem_inc(stored[c], 1)

            def halves(dram, b, c):
                return dram[b, 4 * c:4 * c + 4].rearrange("t p c -> p t c")

            def load_x(b, c):
                sp.dma_start((x_in, x_late)[c][:, :, :], halves(x_t, b, c)).then_inc(x_loaded[c], 16)

            def load_y(b, c):
                sp.wait_ge(stored[c], 16 * b + 1)
                stand_alone(sp, "sp")
                sp.dma_start((y, x_in)[c][:, :, :], halves(x_t, b, c)).then_inc(y_in[c], 16)

            def stack(parts, dst, h, signal):
                rows = slice(HEAD_DIM * h, HEAD_DIM * (h + 1))
                for r, part in enumerate(parts):
                    sp.dma_start(dst[HEAD_DIM * r:HEAD_DIM * (r + 1), h, :].bitcast(F32),
                                 part[rows, :].bitcast(F32)).then_inc(signal, 16)

            def stack_qk(h):
                stack((hi[0], hi[0], lo[0]), q_st, h, stacked[h])
                stack((hi[1], lo[1], hi[1]), k_st, h, stacked[h])

            def stack_g(h):
                stack((hi[2], hi[2], lo[2]), ga_st, h, g_stacked)
                stack((hi[2], lo[2], hi[2]), gb_st, h, g_stacked)

            def stacks_free(u):
                sp.wait_ge(k_split, u + 1)
                stand_alone(sp, "sp")
                sp.wait_ge(st_mm, u * NT * NC + 1)
                stand_alone(sp, "sp")

            def g_stacks_free(u):
                sp.wait_ge(g_split, u + 1)
                stand_alone(sp, "sp")
                sp.wait_ge(gg_mm, u * NT * NC + 1)
                stand_alone(sp, "sp")

            def load_lse(b, g, more, h):
                wait_side(sp, side_free, b, g, more, "lse", h)
                stand_alone(sp, "sp")
                for r, part in enumerate((lse_hi, lse_lo)):
                    sp.dma_start(q_st[SPLIT + r:SPLIT + r + 1, h, :].bitcast(F32).rearrange("o (t n) -> o t n", n=P),
                                 part[:, :].bitcast(F32)).then_inc(lse_in[h], 16)

            for c in range(NC):
                load_x(0, c)
            sp.wait_ge(k_split, 1)
            for h in range(HG):
                stack_qk(h)

            def scores(b, g, more):
                u = b * GROUPS + g
                if g > 0:
                    stacks_free(u)
                    stack_qk(0)
                    if g == GROUPS - 1 and more:
                        sp.wait_ge(av_ev, u + 1)
                        stand_alone(sp, "sp")
                        load_x(b + 1, 1)
                    for h in range(1, HG):
                        stack_qk(h)
                g_stacks_free(u)
                stack_g(0)
                load_lse(b, g, more, 0)
                stack_g(1)
                stack_g(2)
                load_lse(b, g, more, 1)
                stack_g(3)
                load_lse(b, g, more, 2)
                if g == GROUPS - 2 and more:
                    sp.wait_ge(stored[1], 16 * b + 1)
                    stand_alone(sp, "sp")
                    load_x(b + 1, 0)
                if g == GROUPS - 1:
                    load_y(b, 0)
                    if more:
                        wait_side(sp, side_mm, b, g, more, "x", 3)
                        stand_alone(sp, "sp")
                    load_y(b, 1)
                load_lse(b, g, more, 3)

            def post(b, more):
                if more:
                    u = b * GROUPS + GROUPS
                    stacks_free(u)
                    for h in range(HG):
                        stack_qk(h)
                for c in range(NC):
                    sp.wait_ge(out_ok, b * TT + 4 * c + 5)
                    stand_alone(sp, "sp")
                    sp.dma_start(halves(out_t, b, c), (y, x_in)[c][:, :, :]).then_inc(stored[c], 16)

            run(sp, lambda *a: None, scores, lambda *a: None, post)
            for c in range(NC):
                sp.wait_ge(stored[c], 16 * BATCH + 1)

        @block.gpsimd
        def _(pool):
            pool.memset(ident[:, :], 0.0).then_inc(pool_step, 1)
            pool.sem_inc(vc_ok, 1)
            pool.memset(minus_half[:, :], -0.5).then_inc(pool_step, 1)
            pool.memset(eps1[:, :], 1e-6).then_inc(pool_step, 1)
            pool.memset(eps2[:, :], 1e-5).then_inc(pool_step, 1)
            pool.memset(gw[:, :, :], 0.0).then_inc(const_ok, 1)
            pool.wait_ge(pool_step, 4)
            pool.affine_select(out=ident[:, :], in_=ident[:, :], compare_op=ALU.not_equal, fill=1.0, base=0,
                               pattern=[[-1, P]], channel_multiplier=1).then_inc(ident_ok, 1)
            pool.wait_ge(weights_in, 16 * 7)
            pool.tensor_copy(fc1_s[:, :], fc1_raw[:, :]).then_inc(fc1_ok, 1)
            pool.wait_ge(fc1_ok, 1)
            pool.tensor_tensor(fc1_s[64:P, :], fc1_raw[64:P, :], fc1_s[64:P, :].bitcast(F32),
                               ALU.subtract).then_inc(fc1_ok, 1)
            pool.wait_ge(fc1_ok, 2)

            def x_inverse_std(b, t):
                n = b * TT + t + 1
                pool.wait_ge(x_stat, n)
                pool.tensor_tensor(x_var[:, t:t + 1], x_stats_s[:, t, 7:8], eps1[:, :], ALU.add).then_inc(x_var_ok, 1)
                pool.wait_ge(x_var_ok, n)
                pool.tensor_tensor(x_rstd[:, t:t + 1], x_var[:, t:t + 1], minus_half[:, 0:1],
                                   ALU.pow).then_inc(x_rstd_ok, 1)

            def split(i, whole, u, n, done):
                stand_alone(pool, "pool")
                pool.tensor_copy(hi[i][:, :], whole[:, :]).then_inc(split_hi, 1)
                pool.wait_ge(split_hi, u * 3 + n + 1)
                pool.tensor_tensor(lo[i][:, :], whole[:, :], hi[i][:, :].bitcast(F32), ALU.subtract).then_inc(done, 1)

            def prepare(b, g, more, u):
                for part in range(2):
                    wait_side(pool, side_free, b, g, more, "q", part)
                if b is not None:
                    for h in range(HG):
                        pool.wait_ge(stacked[h], u * 6 * 16)
                split(0, src, u, 0, q_split)
                pool.wait_ge(g_rec, u + 1)
                pool.tensor_tensor(gw[:, :, 0:GP_NUM], gw[:, :, 0:GP_NUM],
                                   grec[:, :].unsqueeze(2).broadcast_to([P, NT, GP_NUM]), ALU.mult).then_inc(g_ok, 1)
                for part in range(2):
                    wait_side(pool, side_free, b, g, more, "k", part)
                split(1, k_src, u, 1, k_split)

            for t in range(TT):
                x_inverse_std(0, t)
            prepare(None, 0, True, 0)

            def scores(b, g, more):
                u = b * GROUPS + g
                for part in range(2):
                    wait_side(pool, side_free, b, g, more, "g", part)
                split(2, src, u, 2, g_split)
                if g == GROUPS - 1 and more:
                    for t in range(4, TT):
                        x_inverse_std(b + 1, t)
                if more or g < GROUPS - 1:
                    prepare(b, g, more, u + 1)

            def products(b, g, more):
                u = b * GROUPS + g
                for part in range(2):
                    wait_side(pool, side_free, b, g, more, "v", part)
                for m in range(TT):
                    pool.wait_ge(c_ok, u * TT + m + 1)
                    if m >= 2:
                        pool.wait_ge(av_mm, (u * TT + m - 1) * NC)
                    pool.tensor_tensor(vc[:, m % 2, :, :],
                                       v_s[:, m * P:(m + 1) * P].rearrange("p (h d) -> p h d", h=HG),
                                       crec[:, m % 2, :].unsqueeze(2).broadcast_to([P, HG, HEAD_DIM]),
                                       ALU.mult).then_inc(vc_ok, 1)
                    if g == GROUPS - 2 and more and 1 <= m <= 4:
                        x_inverse_std(b + 1, m - 1)

            def post(b, more):
                for c in range(NC):
                    n = b * NC + c
                    pool.wait_ge(y_stat, 4 * n + 4)
                    pool.tensor_tensor(y_var[:, :], y_stats_s[:, :, 7], eps2[:, :], ALU.add).then_inc(y_var_ok, 1)
                    pool.wait_ge(y_var_ok, n + 1)
                    pool.tensor_tensor(y_rstd[:, :], y_var[:, :], minus_half[:, :], ALU.pow).then_inc(y_rstd_ok, 1)

            run(pool, lambda *a: None, scores, products, post)

        @block.scalar
        def _(act):
            act.wait_ge(t_dve, 1)
            act.activation(tpar[:, 2:3], tpar[:, 1:2], ACT.Exp).then_inc(t_exp, 1)
            act.wait_ge(t_exp, 1)
            act.activation(tpar[:, 3:4], tpar[:, 2:3], ACT.Ln, bias=1.0).then_inc(t_act, 1)
            act.sem_inc(av_ev, 1)
            act.preload_act_table_set("natural_log_exp_and_others")

            def side(b, g, more, n, what, part, u):
                bank = side_bank(b, g, n)
                psb = ps[:, 6 + bank, :]
                half = slice(part * CH, (part + 1) * CH)
                if what == "logit":
                    if part == 1:
                        for w in range(2):
                            wait_side(act, side_free, b, g, more, "logit", w)
                        if b is None:
                            act.wait_ge(t_dve, 4)
                        act.activation(gw[:, :, 0:GP_NUM], gw[:, :, 0:GP_NUM], ACT.Exp,
                                       scale=tpar[:, 6:7]).then_inc(g_exp, 1)
                    return
                if what == "lse":
                    return
                act.wait_ge(side_mm[bank], side_count(b, g, n) + 1)
                if what == "x":
                    act.copy(xn_t[:, :, part * P:(part + 1) * P],
                             psb[:, 0:DIM].rearrange("p (k n) -> p k n", k=KC)).then_inc(side_free[bank], 1)
                elif what == "q":
                    if part == 0 and b is not None:
                        act.wait_ge(g_split, u)
                    act.mul(src[:, half], psb, SCALE).then_inc(side_free[bank], 1)
                elif what == "k":
                    act.copy(k_src[:, half], psb).then_inc(side_free[bank], 1)
                elif what == "v":
                    act.copy(v_s[:, half], psb).then_inc(side_free[bank], 1)
                elif what == "g":
                    if part == 0:
                        act.wait_ge(q_split, u)
                    act.copy(src[:, half], psb).then_inc(side_free[bank], 1)

            def scores(b, g, more):
                u = b * GROUPS + g
                for i in range(NT):
                    act.wait_ge(s_max, u * NT + i + 1)
                    act.activation(wide(i % 3), wide(i % 3), ACT.Exp, bias=neg_max[:, i:i + 1],
                                   accum_out=row_sum[:, i:i + 1]).then_inc(s_exp, 1)
                    if i % TT == TT - 1:
                        h = i // TT
                        act.wait_ge(s_exp, u * NT + i + 1)
                        act.activation(log_sum[:, TT * h:TT * (h + 1)], row_sum[:, TT * h:TT * (h + 1)],
                                       ACT.Ln).then_inc(s_log, 1)
                    between(lambda what: 1 if what == "logit" else -1, i, side, b, g, more, u)

            def products(b, g, more):
                u = b * GROUPS + g
                for i in range(NT):
                    for c in range(NC):
                        act.wait_ge(st_mm, (u * NT + i) * NC + c + 2)
                        if i >= 2 * HG and i % HG == 0 and c == 0:
                            act.wait_ge(av_mm, (u * TT + i // HG - 1) * NC)
                        if i == 2 * HG - 1 and c == 0 and (more or g < GROUPS - 1):
                            act.wait_ge(k_split, u + 2)
                        act.activation(attn[:, i % (2 * HG), c * CH:(c + 1) * CH], ps[:, (NC * i + c) % 3, :],
                                       ACT.Exp).then_inc(st_exp, 1)
                act.wait_ge(av_mm, (u + 1) * TT * NC)
                act.copy(attn_t[:, g, :], wide(3)).then_inc(av_ev, 1)

            def post(b, more):
                for c in range(NC):
                    bc = b * NC + c
                    act.wait_ge(z_tp, bc + 1)
                    act.copy(z_s[0:KRON, :], ps[0:KRON, 4, :]).then_inc(zh_ok, 1)
                    act.copy(z_s[2 * KRON:3 * KRON, :], ps[0:KRON, 4, :]).then_inc(zh_ok, 1)
                    for f in range(FB):
                        act.wait_ge(h_mm, bc * FB + f + 1)
                        if f >= 2 * HG:
                            act.wait_ge(p_mm, bc * KC + f // 4 - 1)
                        act.activation(attn[:, f % (2 * HG), 0:CH], ps[:, 5 + f % 2, :], ACT.Gelu).then_inc(h_ok, 1)
                    act.wait_ge(p_mm, (bc + 1) * KC)
                    act.copy(mlp_part[:, :], ps[:, 7, :]).then_inc(p_ev, 1)
                act.preload_act_table_set("natural_log_exp_and_others")

            run(act, side, scores, products, post)

        @block.tensor
        def _(pe):
            pe.wait_ge(ident_ok, 1)
            pe.wait_ge(const_ok, 2)
            pe.wait_ge(weights_in, 16 * 7)
            pe.wait_ge(fc1_ok, 2)

            pe.sem_inc(st_mm, 1)
            pe.sem_inc(gg_mm, 1)

            def side(b, g, more, n, what, part, u, step, steps):
                bank = side_bank(b, g, n)
                psb = ps[:, 6 + bank, :]
                if step == 0 and not (b is None and n < 2):
                    pe.wait_ge(side_free[bank], side_count(b, g, n))
                gn = 0 if b is None else (g + 1) % GROUPS
                if what == "x":
                    pe.wait_ge(xn_ok, (part + 1) if b is None else (b + 1) * TT + part + 1)
                    tile = (x_in, x_late)[part // 4][:, part % 4, :]
                    for k in range(KC):
                        mm = pe.transpose(psb[:, k * P:(k + 1) * P], tile[:, k * P:(k + 1) * P], ident[:, :])
                elif what in ("q", "k"):
                    if what == "q" and part == 0 and gn == 0 and step == 0:
                        for t in (TT - 2, TT - 1):
                            wait_side(pe, side_free, b, g, more, "x", t)
                    col = (what == "k") * DIM + gn * P
                    for k in range(KC * step // steps, KC * (step + 1) // steps):
                        mm = pe.matmul(psb, wqkv[:, k, col:col + P], xn_t[:, k, part * CH:(part + 1) * CH],
                                       start=(k == 0), stop=(k == KC - 1))
                elif what == "v":
                    for i in range(4 * step // steps, 4 * (step + 1) // steps):
                        t = 4 * part + i
                        for k in range(KC):
                            mm = pe.matmul(psb[:, i * P:(i + 1) * P], xn_t[:, k, t * P:(t + 1) * P],
                                           wqkv[:, k, 2 * DIM + g * P:2 * DIM + (g + 1) * P],
                                           start=(k == 0), stop=(k == KC - 1))
                elif what == "logit":
                    w = HG * GP_NUM
                    if part == 0:
                        for half in range(2):
                            wait_side(pe, side_free, b, g, more, "q", half)
                    for i in range(4):
                        t = 4 * part + i
                        mm = pe.matmul(psb[:, i * w:(i + 1) * w], src[:, t * P:(t + 1) * P], gpb[:, gn, :],
                                       start=True, stop=True)
                elif what == "g":
                    if part == 0:
                        pe.wait_ge(g_ok, u)
                    for i in range(4):
                        t = 4 * part + i
                        mm = pe.transpose(psb[:, i * P:(i + 1) * P],
                                          gw[:, HG * t:HG * (t + 1), :].rearrange("p h m -> p (h m)"), ident[:, :])
                elif what == "lse":
                    pe.wait_ge(lse_ok, (u - 1) * HG + part + 1)
                    mm = pe.transpose(psb[0:TT, 0:P], neg_lse[:, TT * part:TT * (part + 1)], ident[:, :])
                if step == steps - 1:
                    mm.then_inc(side_mm[bank], 1)

            def side_steps(b, g, more, i, u):
                for n, (at, what, part, length) in enumerate(side_work(g, more)):
                    if at <= i < at + length:
                        side(b, g, more, n, what, part, u + 1, i - at, length)

            def scores(b, g, more):
                u = b * GROUPS + g
                if g == 0:
                    pe.wait_ge(out_ok, b * TT + 1)
                for i in range(NT):
                    h, t = i // TT, i % TT
                    if t == 0:
                        pe.wait_ge(stacked[h], (u + 1) * 6 * 16)
                    if i >= 3:
                        pe.wait_ge(s_exp, u * NT + i - 2)
                    for c in range(NC):
                        mm = pe.matmul(ps[:, 2 * (i % 3) + c, :], q_st[0:SPLIT, h, t * P:(t + 1) * P],
                                       k_st[0:SPLIT, h, c * CH:(c + 1) * CH], start=True, stop=True)
                    mm.then_inc(s_mm, 1)
                    if i == 0:
                        pe.wait_ge(av_ev, u + 1)
                    side_steps(b, g, more, i, u)
                side_steps(b, g, more, NT, u)

            def products(b, g, more):
                u = b * GROUPS + g
                pe.wait_ge(s_exp, (u + 1) * NT)
                pe.wait_ge(g_stacked, (u + 1) * 6 * HG * 16)

                def transposed(j):
                    m, h, c = j // (HG * NC), j // NC % HG, j % NC
                    if m == 0 and c == 0:
                        pe.wait_ge(lse_in[h], (u + 1) * 32)
                    if j >= 3:
                        pe.wait_ge(st_exp, u * NT * NC + j - 2)
                    pe.matmul(ps[:, j % 3, :], k_st[:, h, m * P:(m + 1) * P], q_st[:, h, c * CH:(c + 1) * CH],
                              start=True, stop=True).then_inc(st_mm, 1)

                def group_weights(j):
                    m, h, c = j // (HG * NC), j // NC % HG, j % NC
                    if j >= 3:
                        pe.wait_ge(a_ok, u * NT * NC + j - 2)
                    pe.matmul(ps[:, 3 + j % 3, :], ga_st[:, h, m * P:(m + 1) * P], gb_st[:, h, c * CH:(c + 1) * CH],
                              start=True, stop=True).then_inc(gg_mm, 1)

                def weigh_values(m, c):
                    if m == 0 and c == 0:
                        for n in (len(side_work(g, more)) - 2, len(side_work(g, more)) - 1):
                            pe.wait_ge(side_free[side_bank(b, g, n)], side_count(b, g, n) + 1)
                    pe.wait_ge(vc_ok, u * TT + m + 2)
                    for h in range(HG):
                        mm = pe.matmul(ps[HEAD_DIM * h:HEAD_DIM * (h + 1), 6 + c, :], vc[:, m % 2, h, :],
                                       attn[:, HG * (m % 2) + h, c * CH:(c + 1) * CH],
                                       start=(m == 0), stop=(m == TT - 1))
                    mm.then_inc(av_mm, 1)

                last = NT * NC
                transposed(0)
                for j in range(last):
                    if j + 1 < last:
                        transposed(j + 1)
                    group_weights(j)
                    m, r = j // (HG * NC), j % (HG * NC)
                    if m > 0 and r in (4, 6):
                        weigh_values(m - 1, r // 2 - 2)
                for c in range(NC):
                    weigh_values(TT - 1, c)

            def post(b, more):
                def project(c):
                    for i in range(4):
                        t = 4 * c + i
                        for k in range(KC):
                            mm = pe.matmul(ps[:, i, 0:DIM], attn_t[:, k, t * P:(t + 1) * P], wproj[:, k, :],
                                           start=(k == 0), stop=(k == KC - 1))
                        mm.then_inc(pj_mm, 1)

                def transpose_z(c):
                    pe.wait_ge(z_ok, b * NC + c + 1)
                    for i in range(4):
                        mm = pe.transpose(ps[0:KRON, 4, i * P:(i + 1) * P], z[:, i, :], ident[:, :])
                    mm.then_inc(z_tp, 1)

                def mlp(c):
                    bc = b * NC + c
                    pe.wait_ge(zh_ok, 2 * (bc + 1))
                    pe.wait_ge(zl_ok, 2 * (bc + 1))

                    def mlp_out(r):
                        pe.wait_ge(h_ok, bc * FB + 4 * r + 4)
                        for j in range(4):
                            f = 4 * r + j
                            mm = pe.matmul(ps[KRON * j:KRON * (j + 1), 7, :], p1_s[:, f, :],
                                           attn[:, f % (2 * HG), 0:CH], start=(r == 0), stop=(r == FB // 4 - 1))
                        mm.then_inc(p_mm, 1)

                    for f in range(FB):
                        if f >= 2:
                            pe.wait_ge(h_ok, bc * FB + f - 1)
                        pe.matmul(ps[:, 5 + f % 2, :], fc1_s[:, f * P:(f + 1) * P], z_s[:, :],
                                  start=True, stop=True).then_inc(h_mm, 1)
                        if f % 4 == 1 and f > 4:
                            mlp_out(f // 4 - 1)
                    mlp_out(FB // 4 - 1)

                def spread(c):
                    pe.wait_ge(p_ev, b * NC + c + 1)
                    for i in range(4):
                        pe.matmul(ps[:, i, 0:DIM], mlp_part[:, i * P:(i + 1) * P], p2_s[:, :],
                                  start=True, stop=True).then_inc(e_mm, 1)

                pe.wait_ge(av_ev, (b + 1) * GROUPS + 1)
                project(0)
                transpose_z(0)
                pe.wait_ge(y_ok, b * TT + 4)
                project(1)
                mlp(0)
                transpose_z(1)
                pe.wait_ge(y_ok, b * TT + 8)
                spread(0)
                mlp(1)
                pe.wait_ge(out_ok, b * TT + 5)
                spread(1)

            for n, (_, what, part, _) in enumerate(FIRST):
                side(None, 0, True, n, what, part, 0, 0, 1)
            run(pe, lambda *a: None, scores, products, post)

        @block.vector
        def _(dve):
            dve.memset(k_st[SPLIT:AUG, :, :].bitcast(F32), 1.0).then_inc(const_ok, 1)
            dve.sem_inc(out_ok, 1)
            dve.wait_ge(t_in, 16)
            dve.tensor_scalar(tpar[:, 7:8], tpar[:, 0:1], -1.0, None, ALU.mult).then_inc(t_neg, 1)
            dve.wait_ge(t_neg, 1)
            dve.tensor_tensor(tpar[:, 1:2], tpar[:, 0:1], tpar[:, 7:8], ALU.min).then_inc(t_dve, 1)
            dve.wait_ge(t_act, 1)
            dve.scalar_tensor_tensor(tpar[:, 4:5], tpar[:, 0:1], 0.0, tpar[:, 3:4], ALU.max, ALU.add).then_inc(t_dve, 1)
            dve.wait_ge(t_dve, 2)
            dve.tensor_scalar(tpar[:, 5:6], tpar[:, 4:5], SCALE, None, ALU.mult).then_inc(t_dve, 1)
            dve.wait_ge(t_dve, 3)
            dve.reciprocal(tpar[:, 6:7], tpar[:, 5:6]).then_inc(t_dve, 1)

            steps = {"first": TT + 3, "batch": TT + GROUPS * (3 + TT) + NC * 9, "base": 0, "n": 0}

            def mark(ins):
                steps["n"] += 1
                ins.then_inc(dve_step, 1)

            def settle():
                dve.wait_ge(dve_step, steps["base"] + steps["n"])

            def step(ins):
                mark(ins)
                settle()

            def x_tile(t):
                return (x_in, x_late)[t // 4][:, t % 4, :]

            def x_stats(b, t):
                if t % 4 == 0:
                    dve.wait_ge(x_loaded[t // 4], 16 * (b + 1))
                step(dve.bn_stats(x_stats_s[:, t, 0:6], x_tile(t)))
                stand_alone(dve, "dve")
                dve.bn_aggr(x_stats_s[:, t, 6:8], x_stats_s[:, t, 0:6]).then_inc(x_stat, 1)

            def norm_x(b, t):
                dve.wait_ge(x_rstd_ok, b * TT + t + 1)
                dve.tensor_scalar(x_tile(t), x_tile(t), x_stats_s[:, t, 6:7], x_rstd[:, t:t + 1],
                                  ALU.subtract, ALU.mult).then_inc(xn_ok, 1)

            def side(b, g, more, n, what, part, u):
                bank = side_bank(b, g, n)
                psb = ps[:, 6 + bank, :]
                if what == "x":
                    if b is None:
                        x_stats(0, part)
                        norm_x(0, part)
                elif what == "logit":
                    dve.wait_ge(side_mm[bank], side_count(b, g, n) + 1)
                    w = NT // 2
                    logits = psb[:, 0:w * GP_NUM].rearrange("p (a m) -> p a m", m=GP_NUM)
                    step(dve.tensor_reduce(gmax[:, w * part:w * (part + 1)], logits, X, ALU.max))
                    dve.tensor_tensor(gw[:, w * part:w * (part + 1), 0:GP_NUM], logits,
                                      gmax[:, w * part:w * (part + 1)].unsqueeze(2).broadcast_to([P, w, GP_NUM]),
                                      ALU.subtract).then_inc(side_free[bank], 1)
                elif what == "k" and part == 0:
                    dve.wait_ge(g_exp, u + 1)
                    step(dve.tensor_reduce(gsum[:, :], gw[:, :, 0:GP_NUM], X, ALU.add))
                    dve.reciprocal(grec[:, :], gsum[:, :]).then_inc(g_rec, 1)
                elif what == "lse":
                    dve.wait_ge(side_mm[bank], side_count(b, g, n) + 1)
                    if part > 0:
                        dve.wait_ge(lse_in[part - 1], u * 32)
                    dve.tensor_copy(lse_hi[:, :], psb[0:TT, 0:P]).then_inc(lse_hi_ok, 1)
                    dve.wait_ge(lse_hi_ok, (u - 1) * HG + part + 1)
                    dve.tensor_tensor(lse_lo[:, :], psb[0:TT, 0:P], lse_hi[:, :].bitcast(F32),
                                      ALU.subtract).then_inc(side_free[bank], 1)

            def scores(b, g, more):
                u = b * GROUPS + g

                def lse(h):
                    cols = slice(TT * h, TT * (h + 1))
                    dve.wait_ge(s_log, u * HG + h + 1)
                    dve.tensor_tensor(neg_lse[:, cols], neg_max[:, cols], log_sum[:, cols],
                                      ALU.subtract).then_inc(lse_ok, 1)

                for i in range(NT):
                    dve.wait_ge(s_mm, u * NT + i + 1)
                    dve.tensor_reduce(neg_max[:, i:i + 1], wide(i % 3), X, ALU.max, negate=True).then_inc(s_max, 1)
                    if i % TT == 2 and i > TT:
                        lse(i // TT - 1)
                    if g == GROUPS - 1 and more:
                        if 4 <= i <= 7:
                            x_stats(b + 1, i)
                        if 5 <= i <= 8:
                            norm_x(b + 1, i - 1)
                    between(lambda what: 2 if what == "k" else 0, i, side, b, g, more, u)
                lse(HG - 1)
                between(lambda what: 0, NT, side, b, g, more, u)

            def products(b, g, more):
                u = b * GROUPS + g
                for i in range(NT):
                    m, h = i // HG, i % HG
                    for c in range(NC):
                        n = (u * NT + i) * NC + c + 1
                        dve.wait_ge(st_exp, n)
                        dve.wait_ge(gg_mm, n + 1)
                        a = attn[:, i % (2 * HG), c * CH:(c + 1) * CH]
                        dve.tensor_tensor_reduce(a, ps[:, 3 + (NC * i + c) % 3, :], a, 1.0, 0.0, ALU.mult, ALU.add,
                                                 csum[:, m % 2, h, c:c + 1]).then_inc(a_ok, 1)
                    if h == HG - 1:
                        dve.wait_ge(a_ok, (u * NT + i + 1) * NC)
                        if m >= 2:
                            dve.wait_ge(vc_ok, u * TT + m)
                        step(dve.scalar_tensor_tensor(crec[:, m % 2, :], csum[:, m % 2, :, 0], 1e-8,
                                                      csum[:, m % 2, :, 1], ALU.add, ALU.add))
                        dve.reciprocal(crec[:, m % 2, :], crec[:, m % 2, :]).then_inc(c_ok, 1)
                        if g == GROUPS - 2 and more:
                            if 1 <= m <= 4:
                                x_stats(b + 1, m - 1)
                            if 2 <= m <= 5:
                                norm_x(b + 1, m - 2)

            def post(b, more):
                def residual(c):
                    bc = b * NC + c
                    yt = (y, x_in)[c]
                    dve.wait_ge(y_in[c], 16 * (b + 1))
                    for i in range(4):
                        dve.wait_ge(pj_mm, bc * 4 + i + 1)
                        dve.tensor_tensor(yt[:, i, :], ps[:, i, 0:DIM], yt[:, i, :], ALU.add).then_inc(y_ok, 1)
                    for i in range(4):
                        dve.wait_ge(y_ok, bc * 4 + i + 1)
                        mark(dve.bn_stats(y_stats_s[:, i, 0:6], yt[:, i, :]))
                    settle()
                    stand_alone(dve, "dve")
                    for i in range(4):
                        dve.bn_aggr(y_stats_s[:, i, 6:8], y_stats_s[:, i, 0:6]).then_inc(y_stat, 1)
                    dve.wait_ge(y_stat, bc * 4 + 4)
                    for i in range(4):
                        mark(dve.scalar_tensor_tensor(yn[:, i, :], yt[:, i, :], y_stats_s[:, i, 6:7], fc2_row[:, :],
                                                      ALU.subtract, ALU.mult))
                    settle()
                    step(dve.tensor_reduce(z[:, :, :], yn[:, :, :].rearrange("p i (j l) -> p i j l", l=KIN),
                                           X, ALU.add))
                    dve.wait_ge(y_rstd_ok, bc + 1)
                    dve.tensor_tensor(z[:, :, :], z[:, :, :], y_rstd[:, :].unsqueeze(2).broadcast_to([P, 4, KRON]),
                                      ALU.mult).then_inc(z_ok, 1)

                def split_z(c):
                    bc = b * NC + c
                    dve.wait_ge(zh_ok, 2 * (bc + 1))
                    for r in (1, 3):
                        dve.tensor_tensor(z_s[KRON * r:KRON * (r + 1), :], ps[0:KRON, 4, :],
                                          z_s[0:KRON, :].bitcast(F32), ALU.subtract).then_inc(zl_ok, 1)

                def output(c):
                    yt = (y, x_in)[c]
                    for i in range(4):
                        dve.wait_ge(e_mm, b * TT + 4 * c + i + 1)
                        dve.tensor_tensor(yt[:, i, :], ps[:, i, 0:DIM], yt[:, i, :], ALU.add).then_inc(out_ok, 1)

                residual(0)
                split_z(0)
                residual(1)
                split_z(1)
                output(0)
                output(1)

            for n, (_, what, part, _) in enumerate(FIRST):
                side(None, 0, True, n, what, part, 0)
            assert steps["n"] == steps["first"], steps

            def batch(b, more):
                steps["base"], steps["n"] = steps["first"] + b * steps["batch"], 0
                for g in range(GROUPS):
                    scores(b, g, more)
                    products(b, g, more)
                post(b, more)

            with dve.Fori(0, BATCH - 1) as b:
                batch(b, True)
                assert steps["n"] == steps["batch"], steps
            batch(BATCH - 1, False)


def kernel(x, L0_conv_W_qkv, L0_conv_gp_w, L0_conv_t_param, L0_conv_W_proj,
           L0_ffn_c_fc_1, L0_ffn_c_fc_2, L0_ffn_c_proj_1, L0_ffn_c_proj_2):
    import numpy as np
    import concourse.bacc as bacc
    from concourse.bass_utils import run_bass_kernel_spmd

    def rows(w):
        w = np.asarray(w)
        return np.ascontiguousarray(w.reshape(-1, P, w.shape[1]).transpose(1, 0, 2))

    gp = np.asarray(L0_conv_gp_w).reshape(GROUPS, HG, GP_NUM, HEAD_DIM)
    blocks = np.zeros((HG, HEAD_DIM, GROUPS, HG, GP_NUM), gp.dtype)
    for j in range(HG):
        blocks[j, :, :, j, :] = gp[:, j].transpose(2, 0, 1)
    spread = np.zeros((4, KRON, KRON, KIN), np.asarray(L0_ffn_c_proj_2).dtype)
    for j in range(KRON):
        spread[:, j, j, :] = np.asarray(L0_ffn_c_proj_2)[:, 0]
    arrays = {
        "x": np.ascontiguousarray(np.asarray(x).reshape(BATCH, TOK, DIM)),
        "w_qkv": rows(L0_conv_W_qkv),
        "w_proj": rows(L0_conv_W_proj),
        "gp_blocks": blocks.reshape(P, GROUPS, HG * GP_NUM),
        "t_param": np.ascontiguousarray(np.broadcast_to(np.asarray(L0_conv_t_param).reshape(1, 1), (P, 1))),
        "fc1": np.ascontiguousarray(np.tile(np.asarray(L0_ffn_c_fc_1).T, (4, 1))),
        "fc2": np.ascontiguousarray(np.broadcast_to(np.tile(np.asarray(L0_ffn_c_fc_2)[0], KRON), (P, DIM))),
        "p1": np.ascontiguousarray(np.asarray(L0_ffn_c_proj_1).reshape(KRON, FB, P).transpose(2, 1, 0)),
        "p2": spread.reshape(P, DIM),
    }
    nc = bacc.Bacc("TRN2", target_bir_lowering=False, num_devices=1)
    args = [nc.dram_tensor(name, a.shape, mybir.dt.from_np(a.dtype), kind="ExternalInput").ap()
            for name, a in arrays.items()]
    args.append(nc.dram_tensor("out", (BATCH, TOK, DIM), F32, kind="ExternalOutput").ap())
    metaformer_layer(nc, *args)
    r = run_bass_kernel_spmd(nc, [arrays], core_ids=[0])
    return r.results[0]["out"].reshape(np.asarray(x).shape)
```

```python
from contextlib import ExitStack

import concourse.bass as bass
from concourse import mybir

F32 = mybir.dt.float32
F32R = mybir.dt.float32r
ALU = mybir.AluOpType
ACT = mybir.ActivationFunctionType
X = mybir.AxisListType.X

P = 128
BATCH, TOK, DIM = 8, 1024, 384
HEAD_DIM, GP_NUM, FF = 32, 20, 1536
HEADS = DIM // HEAD_DIM
HG = P // HEAD_DIM
GROUPS = HEADS // HG
KC = DIM // P
TT = TOK // P
CH = 512
NC = TOK // CH
RING = 12
PIECES = 4
PW = TOK // PIECES
KRON = 32
KIN = DIM // KRON
FB = FF // P
NT = HG * TT
SCALE = float(HEAD_DIM) ** -0.5
SPLIT = 3 * HEAD_DIM
AUG = SPLIT + 2


def metaformer_layer(nc, x, w_qkv, w_proj, gp_blocks, t_param, fc1, fc2, p1, p2, out):
    x_t = x.rearrange("b (t p) c -> b t p c", p=P)
    out_t = out.rearrange("b (t p) c -> b t p c", p=P)

    with ExitStack() as ctx:
        def sb(name, shape, dt=F32):
            return ctx.enter_context(nc.sbuf_tensor(name, shape, dt))

        def sem(name):
            return ctx.enter_context(nc.semaphore(name))

        wqkv = sb("wqkv", [P, KC, 3 * DIM])
        wproj = sb("wproj", [P, KC, DIM])
        gpb = sb("gpb", [P, GROUPS, HG * GP_NUM])
        fc1_s = sb("fc1_s", [P, FF], F32R)
        fc2_row = sb("fc2_row", [P, DIM])
        p1_s = sb("p1_s", [P, FB, KRON])
        p2_s = sb("p2_s", [P, DIM])
        ident = sb("ident", [P, P])
        tpar = sb("tpar", [P, 8])

        x_in = sb("x_in", [P, 4, DIM])
        xn_t = sb("xn_t", [P, KC, TOK])
        attn_t = sb("attn_t", [P, GROUPS, TOK])
        z = sb("z", [P, 4, KRON])
        z_s = sb("z_s", [P, CH], F32R)
        x_stats_s = sb("x_stats_s", [P, TT, 8])
        x_var = sb("x_var", [P, TT])
        x_rstd = sb("x_rstd", [P, TT])
        y_stats_s = sb("y_stats_s", [P, 4, 8])
        y_var = sb("y_var", [P, 4])
        y_rstd = sb("y_rstd", [P, 4])
        minus_half = sb("minus_half", [P, 4])
        eps1 = sb("eps1", [P, 1])
        eps2 = sb("eps2", [P, 4])

        q_hi, q_lo = sb("q_hi", [P, TOK], F32R), sb("q_lo", [P, TOK], F32R)
        k_hi, k_lo = sb("k_hi", [P, TOK], F32R), sb("k_lo", [P, TOK], F32R)
        gw = sb("gw", [P, NT, HEAD_DIM])
        gmax = sb("gmax", [P, NT])
        gsum = sb("gsum", [P, NT])
        grec = sb("grec", [P, NT])
        v_s = sb("v_s", [P, TOK])
        q_st = sb("q_st", [AUG, HG, TOK], F32R)
        k_st = sb("k_st", [AUG, HG, TOK], F32R)
        ga_st = sb("ga_st", [SPLIT, HG, TOK], F32R)
        gb_st = sb("gb_st", [SPLIT, HG, TOK], F32R)
        neg_max = sb("neg_max", [P, NT])
        row_sum = sb("row_sum", [P, NT])
        log_sum = sb("log_sum", [P, NT])
        neg_lse = sb("neg_lse", [P, NT])
        lse_hi = sb("lse_hi", [TT, P], F32R)
        lse_lo = sb("lse_lo", [TT, P], F32R)
        attn = sb("attn", [P, RING, TOK])
        csum = sb("csum", [P, 2, HG])
        crec = sb("crec", [P, 2, HG])
        vc = sb("vc", [P, 2, HG, HEAD_DIM])
        def ring(first, n, width):
            tiles = attn[:, first:first + -(-n * width // TOK), :].rearrange("p a n -> p (a n)")
            return tiles[:, 0:n * width].rearrange("p (i n) -> p i n", n=width)

        fc1_raw = ring(6, 1, FF)[:, 0, :]
        g_hi, g_lo = attn[:, 0, :].bitcast(F32R), attn[:, 1, :].bitcast(F32R)
        x_late = ring(2, 4, DIM)
        y = ring(8, 4, DIM)
        src = attn[:, RING - 2, :]
        k_src = attn[:, RING - 1, :]
        hi, lo = [q_hi, k_hi, g_hi], [q_lo, k_lo, g_lo]
        yn = attn[:, 0:4, CH:CH + DIM]
        mlp_part = attn[:, 6, CH:2 * CH]

        ps = ctx.enter_context(nc.psum_tensor("ps", [P, 8, CH], F32))

        def wide(slot):
            return ps[:, 2 * slot:2 * slot + 2, :].rearrange("p a n -> p (a n)")

        qkv_in, weights_in, t_in, ident_ok, const_ok = sem("qkv_in"), sem("weights_in"), sem("t_in"), sem("ident_ok"), sem("const_ok")
        t_neg, t_exp, t_act, t_dve, fc1_ok = sem("t_neg"), sem("t_exp"), sem("t_act"), sem("t_dve"), sem("fc1_ok")
        x_loaded = [sem("x_loaded0"), sem("x_loaded1")]
        x_stat, x_var_ok, x_rstd_ok, xn_ok = sem("x_stat"), sem("x_var_ok"), sem("x_rstd_ok"), sem("xn_ok")
        side_mm = [sem("side_mm0"), sem("side_mm1")]
        side_free = [sem("side_free0"), sem("side_free1")]
        split_hi, q_split, k_split, g_split = sem("split_hi"), sem("q_split"), sem("k_split"), sem("g_split")
        stacked = [sem(f"stacked{h}") for h in range(HG)]
        g_exp, g_rec, g_ok, g_stacked = sem("g_exp"), sem("g_rec"), sem("g_ok"), sem("g_stacked")
        s_mm, s_max, s_exp, s_log = sem("s_mm"), sem("s_max"), sem("s_exp"), sem("s_log")
        lse_ok, lse_hi_ok = sem("lse_ok"), sem("lse_hi_ok")
        lse_in = [sem(f"lse_in{h}") for h in range(HG)]
        st_mm, st_exp, gg_mm, a_ok, c_ok, vc_ok = sem("st_mm"), sem("st_exp"), sem("gg_mm"), sem("a_ok"), sem("c_ok"), sem("vc_ok")
        av_mm, av_ev = sem("av_mm"), sem("av_ev")
        y_in = [sem("y_loaded0"), sem("y_loaded1")]
        pj_mm, y_ok, y_stat, y_var_ok, y_rstd_ok, z_ok = sem("pj_mm"), sem("y_ok"), sem("y_stat"), sem("y_var_ok"), sem("y_rstd_ok"), sem("z_ok")
        z_tp, zh_ok, zl_ok = sem("z_tp"), sem("zh_ok"), sem("zl_ok")
        h_mm, h_ok, p_mm, p_ev, e_mm, out_ok = sem("h_mm"), sem("h_ok"), sem("p_mm"), sem("p_ev"), sem("e_mm"), sem("out_ok")
        stored = [sem("stored0"), sem("stored1")]
        dve_step, pool_step = sem("dve_step"), sem("pool_step")
        passed = {"sp": sem("sp_passed"), "pool": sem("pool_passed"), "dve": sem("dve_passed")}

        def stand_alone(engine, name):
            engine.sem_inc(passed[name], 1)

        def side_work(g, more):
            if g < GROUPS - 1:
                return [(2, "g", 0, 1), (3, "g", 1, 1), (4, "v", 0, 3), (7, "v", 1, 3), (10, "q", 0, 3),
                        (13, "q", 1, 3), (14, "lse", 0, 1), (17, "logit", 0, 1), (18, "logit", 1, 1),
                        (19, "k", 0, 3), (22, "lse", 1, 1), (23, "k", 1, 3), (30, "lse", 2, 1), (NT, "lse", 3, 1)]
            if more:
                return ([(2, "g", 0, 1), (3, "g", 1, 1), (4, "v", 0, 2), (6, "v", 1, 2)] +
                        [(8 + t, "x", t, 1) for t in range(TT)] +
                        [(16, "lse", 0, 1), (17, "q", 0, 2), (19, "q", 1, 2), (22, "logit", 0, 1),
                         (23, "logit", 1, 1), (24, "lse", 1, 1), (25, "k", 0, 2), (27, "k", 1, 2),
                         (30, "lse", 2, 1), (NT, "lse", 3, 1)])
            return [(2, "g", 0, 1), (3, "g", 1, 1), (4, "v", 0, 4), (8, "v", 1, 4), (14, "lse", 0, 1),
                    (22, "lse", 1, 1), (30, "lse", 2, 1), (NT, "lse", 3, 1)]

        FIRST = [(0, "x", t, 1) for t in range(TT)] + [(0, w, i, 1) for w in ("q", "logit", "k") for i in range(2)]
        PER_BATCH = [len(side_work(g, True)) for g in range(GROUPS)]
        BEFORE = [sum(PER_BATCH[:g]) for g in range(GROUPS)]

        def side_count(b, g, n):
            if b is None:
                return n // 2
            return len(FIRST) // 2 + b * (sum(PER_BATCH) // 2) + (BEFORE[g] + n) // 2

        def side_bank(b, g, n):
            return n % 2 if b is None else (BEFORE[g] + n) % 2

        def wait_side(engine, signal, b, g, more, what, part):
            work = FIRST if b is None else side_work(g, more)
            n = [w[1:3] for w in work].index((what, part))
            engine.wait_ge(signal[side_bank(b, g, n)], side_count(b, g, n) + 1)

        def run(engine, side, scores, products, post):
            for n, (_, what, part, _) in enumerate(FIRST):
                side(None, 0, True, n, what, part, 0)

            def batch(b, more):
                for g in range(GROUPS):
                    scores(b, g, more)
                    products(b, g, more)
                post(b, more)

            with engine.Fori(0, BATCH - 1) as b:
                batch(b, True)
            batch(BATCH - 1, False)

        def between(lag, i, side, b, g, more, u):
            for n, (at, what, part, length) in enumerate(side_work(g, more)):
                due = min(max(at + length - 1 + lag(what), 0), NT - 1) if at < NT else NT
                if due == i:
                    side(b, g, more, n, what, part, u + 1)

        block = ctx.enter_context(nc.Block())

        @block.sync
        def _(sp):
            sp.dma_start(x_in[:, :, :], x_t[0, 0:4].rearrange("t p c -> p t c")).then_inc(x_loaded[0], 16)
            sp.dma_start(tpar[:, 0:1], t_param).then_inc(t_in, 16)
            sp.dma_start(x_late[:, :, :], x_t[0, 4:8].rearrange("t p c -> p t c")).then_inc(x_loaded[1], 16)
            for dst, src_ in ((wqkv[:, :, :], w_qkv), (gpb[:, :, :], gp_blocks)):
                sp.dma_start(dst, src_).then_inc(qkv_in, 16)
            for dst, src_ in ((wproj[:, :, :], w_proj), (fc1_raw[:, :], fc1), (fc2_row[:, :], fc2),
                              (p1_s[:, :, :], p1), (p2_s[:, :], p2)):
                sp.dma_start(dst, src_).then_inc(weights_in, 16)
            for c in range(NC):
                sp.sem_inc(stored[c], 1)

            def halves(dram, b, c):
                return dram[b, 4 * c:4 * c + 4].rearrange("t p c -> p t c")

            def load_x(b, c):
                sp.dma_start((x_in, x_late)[c][:, :, :], halves(x_t, b, c)).then_inc(x_loaded[c], 16)

            def load_y(b, c):
                sp.wait_ge(stored[c], 16 * b + 1)
                stand_alone(sp, "sp")
                sp.dma_start((y, x_in)[c][:, :, :], halves(x_t, b, c)).then_inc(y_in[c], 16)

            def stack(parts, dst, h, signal):
                rows = slice(HEAD_DIM * h, HEAD_DIM * (h + 1))
                for r, part in enumerate(parts):
                    sp.dma_start(dst[HEAD_DIM * r:HEAD_DIM * (r + 1), h, :].bitcast(F32),
                                 part[rows, :].bitcast(F32)).then_inc(signal, 16)

            def stack_qk(h):
                stack((hi[0], hi[0], lo[0]), q_st, h, stacked[h])
                stack((hi[1], lo[1], hi[1]), k_st, h, stacked[h])

            def stack_g(h):
                stack((hi[2], hi[2], lo[2]), ga_st, h, g_stacked)
                stack((hi[2], lo[2], hi[2]), gb_st, h, g_stacked)

            def restack_qk(u, h):
                if h == 0:
                    sp.wait_ge(k_split, u + 1)
                    stand_alone(sp, "sp")
                sp.wait_ge(st_mm, u * NT * NC - NC * (HG - 1 - h) + 1)
                stand_alone(sp, "sp")
                stack_qk(h)

            def g_stacks_free(u):
                sp.wait_ge(g_split, u + 1)
                stand_alone(sp, "sp")
                sp.wait_ge(gg_mm, u * NT + 1)
                stand_alone(sp, "sp")

            def load_lse(b, g, more, h):
                wait_side(sp, side_free, b, g, more, "lse", h)
                stand_alone(sp, "sp")
                for r, part in enumerate((lse_hi, lse_lo)):
                    sp.dma_start(q_st[SPLIT + r:SPLIT + r + 1, h, :].bitcast(F32).rearrange("o (t n) -> o t n", n=P),
                                 part[:, :].bitcast(F32)).then_inc(lse_in[h], 16)

            sp.wait_ge(k_split, 1)
            for h in range(HG):
                stack_qk(h)

            def scores(b, g, more):
                u = b * GROUPS + g
                if g > 0:
                    restack_qk(u, 0)
                    if g == GROUPS - 1 and more:
                        sp.wait_ge(av_mm, (u * TT - 1) * PIECES)
                        stand_alone(sp, "sp")
                        load_x(b + 1, 1)
                    for h in range(1, HG):
                        restack_qk(u, h)
                g_stacks_free(u)
                stack_g(0)
                load_lse(b, g, more, 0)
                stack_g(1)
                stack_g(2)
                load_lse(b, g, more, 1)
                stack_g(3)
                load_lse(b, g, more, 2)
                if g == GROUPS - 2 and more:
                    sp.wait_ge(stored[1], 16 * b + 1)
                    stand_alone(sp, "sp")
                    load_x(b + 1, 0)
                if g == GROUPS - 1:
                    if more:
                        wait_side(sp, side_mm, b, g, more, "x", 3)
                        stand_alone(sp, "sp")
                    load_y(b, 1)
                load_lse(b, g, more, 3)

            def post(b, more):
                sp.wait_ge(av_mm, (b + 1) * GROUPS * TT * PIECES)
                stand_alone(sp, "sp")
                load_y(b, 0)
                if more:
                    for h in range(HG):
                        restack_qk(b * GROUPS + GROUPS, h)
                for c in range(NC):
                    sp.wait_ge(out_ok, b * TT + 4 * c + 5)
                    stand_alone(sp, "sp")
                    sp.dma_start(halves(out_t, b, c), (y, x_in)[c][:, :, :]).then_inc(stored[c], 16)

            run(sp, lambda *a: None, scores, lambda *a: None, post)
            for c in range(NC):
                sp.wait_ge(stored[c], 16 * BATCH + 1)

        @block.gpsimd
        def _(pool):
            pool.memset(ident[:, :], 0.0).then_inc(pool_step, 1)
            pool.sem_inc(vc_ok, 1)
            pool.memset(minus_half[:, :], -0.5).then_inc(pool_step, 1)
            pool.memset(eps1[:, :], 1e-6).then_inc(pool_step, 1)
            pool.memset(eps2[:, :], 1e-5).then_inc(pool_step, 1)
            pool.memset(gw[:, :, :], 0.0).then_inc(const_ok, 1)
            pool.wait_ge(pool_step, 4)
            pool.affine_select(out=ident[:, :], in_=ident[:, :], compare_op=ALU.not_equal, fill=1.0, base=0,
                               pattern=[[-1, P]], channel_multiplier=1).then_inc(ident_ok, 1)
            def x_inverse_std(b, t):
                n = b * TT + t + 1
                pool.wait_ge(x_stat, n)
                pool.tensor_tensor(x_var[:, t:t + 1], x_stats_s[:, t, 7:8], eps1[:, :], ALU.add).then_inc(x_var_ok, 1)
                pool.wait_ge(x_var_ok, n)
                pool.tensor_tensor(x_rstd[:, t:t + 1], x_var[:, t:t + 1], minus_half[:, 0:1],
                                   ALU.pow).then_inc(x_rstd_ok, 1)

            def split(i, whole, u, n, done):
                stand_alone(pool, "pool")
                pool.tensor_copy(hi[i][:, :], whole[:, :]).then_inc(split_hi, 1)
                pool.wait_ge(split_hi, u * 3 + n + 1)
                pool.tensor_tensor(lo[i][:, :], whole[:, :], hi[i][:, :].bitcast(F32), ALU.subtract).then_inc(done, 1)

            def prepare(b, g, more, u):
                for part in range(2):
                    wait_side(pool, side_free, b, g, more, "q", part)
                if b is not None:
                    for h in range(HG):
                        pool.wait_ge(stacked[h], u * 6 * 16)
                split(0, src, u, 0, q_split)
                pool.wait_ge(g_rec, u + 1)
                pool.tensor_tensor(gw[:, :, 0:GP_NUM], gw[:, :, 0:GP_NUM],
                                   grec[:, :].unsqueeze(2).broadcast_to([P, NT, GP_NUM]), ALU.mult).then_inc(g_ok, 1)
                for part in range(2):
                    wait_side(pool, side_free, b, g, more, "k", part)
                split(1, k_src, u, 1, k_split)

            for t in range(TT):
                x_inverse_std(0, t)
            prepare(None, 0, True, 0)
            pool.wait_ge(weights_in, 16 * 5)
            pool.tensor_copy(fc1_s[:, :], fc1_raw[:, :]).then_inc(fc1_ok, 1)
            pool.wait_ge(fc1_ok, 1)
            pool.tensor_tensor(fc1_s[64:P, :], fc1_raw[64:P, :], fc1_s[64:P, :].bitcast(F32),
                               ALU.subtract).then_inc(fc1_ok, 1)
            pool.wait_ge(fc1_ok, 2)

            def scores(b, g, more):
                u = b * GROUPS + g
                for part in range(2):
                    wait_side(pool, side_free, b, g, more, "g", part)
                split(2, src, u, 2, g_split)
                if g == GROUPS - 1 and more:
                    for t in range(4, TT):
                        x_inverse_std(b + 1, t)
                if more or g < GROUPS - 1:
                    prepare(b, g, more, u + 1)

            def products(b, g, more):
                u = b * GROUPS + g
                for part in range(2):
                    wait_side(pool, side_free, b, g, more, "v", part)
                for m in range(TT):
                    pool.wait_ge(c_ok, u * TT + m + 1)
                    if m >= 2:
                        pool.wait_ge(av_mm, (u * TT + m - 1) * PIECES)
                    pool.tensor_tensor(vc[:, m % 2, :, :],
                                       v_s[:, m * P:(m + 1) * P].rearrange("p (h d) -> p h d", h=HG),
                                       crec[:, m % 2, :].unsqueeze(2).broadcast_to([P, HG, HEAD_DIM]),
                                       ALU.mult).then_inc(vc_ok, 1)
                    if g == GROUPS - 2 and more and 1 <= m <= 4:
                        x_inverse_std(b + 1, m - 1)

            def post(b, more):
                for c in range(NC):
                    n = b * NC + c
                    pool.wait_ge(y_stat, 4 * n + 4)
                    pool.tensor_tensor(y_var[:, :], y_stats_s[:, :, 7], eps2[:, :], ALU.add).then_inc(y_var_ok, 1)
                    pool.wait_ge(y_var_ok, n + 1)
                    pool.tensor_tensor(y_rstd[:, :], y_var[:, :], minus_half[:, :], ALU.pow).then_inc(y_rstd_ok, 1)

            run(pool, lambda *a: None, scores, products, post)

        @block.scalar
        def _(act):
            act.wait_ge(t_dve, 1)
            act.activation(tpar[:, 2:3], tpar[:, 1:2], ACT.Exp).then_inc(t_exp, 1)
            act.wait_ge(t_exp, 1)
            act.activation(tpar[:, 3:4], tpar[:, 2:3], ACT.Ln, bias=1.0).then_inc(t_act, 1)
            act.sem_inc(av_ev, 1)
            act.preload_act_table_set("natural_log_exp_and_others")

            def side(b, g, more, n, what, part, u):
                bank = side_bank(b, g, n)
                psb = ps[:, 6 + bank, :]
                half = slice(part * CH, (part + 1) * CH)
                if what == "logit":
                    if part == 1:
                        for w in range(2):
                            wait_side(act, side_free, b, g, more, "logit", w)
                        if b is None:
                            act.wait_ge(t_dve, 4)
                        act.activation(gw[:, :, 0:GP_NUM], gw[:, :, 0:GP_NUM], ACT.Exp,
                                       scale=tpar[:, 6:7]).then_inc(g_exp, 1)
                    return
                if what == "lse":
                    return
                act.wait_ge(side_mm[bank], side_count(b, g, n) + 1)
                if what == "x":
                    act.copy(xn_t[:, :, part * P:(part + 1) * P],
                             psb[:, 0:DIM].rearrange("p (k n) -> p k n", k=KC)).then_inc(side_free[bank], 1)
                elif what == "q":
                    if part == 0 and b is not None:
                        act.wait_ge(g_split, u)
                    act.mul(src[:, half], psb, SCALE).then_inc(side_free[bank], 1)
                elif what == "k":
                    act.copy(k_src[:, half], psb).then_inc(side_free[bank], 1)
                elif what == "v":
                    act.copy(v_s[:, half], psb).then_inc(side_free[bank], 1)
                elif what == "g":
                    if part == 0:
                        act.wait_ge(q_split, u)
                    act.copy(src[:, half], psb).then_inc(side_free[bank], 1)

            def take_output(b, g):
                act.wait_ge(av_mm, (b * GROUPS + g + 1) * TT * PIECES)
                act.copy(attn_t[:, g, :], wide(3)).then_inc(av_ev, 1)

            def scores(b, g, more):
                u = b * GROUPS + g
                for i in range(NT):
                    act.wait_ge(s_max, u * NT + i + 1)
                    act.activation(wide(i % 3), wide(i % 3), ACT.Exp, bias=neg_max[:, i:i + 1],
                                   accum_out=row_sum[:, i:i + 1]).then_inc(s_exp, 1)
                    if i == 0 and g > 0:
                        take_output(b, g - 1)
                    if i % TT == TT - 1:
                        h = i // TT
                        act.wait_ge(s_exp, u * NT + i + 1)
                        act.activation(log_sum[:, TT * h:TT * (h + 1)], row_sum[:, TT * h:TT * (h + 1)],
                                       ACT.Ln).then_inc(s_log, 1)
                    between(lambda what: 1 if what == "logit" else -1, i, side, b, g, more, u)

            def products(b, g, more):
                u = b * GROUPS + g
                for i in range(NT):
                    for c in range(NC):
                        act.wait_ge(st_mm, (u * NT + i) * NC + c + 2)
                        if i >= RING and (i - RING) % HG == 0 and c == 0:
                            act.wait_ge(av_mm, (u * TT + (i - RING) // HG + 1) * PIECES)
                        if i == 8 and c == 0 and g == 0:
                            act.wait_ge(stored[0], 16 * b + 1)
                        if i == RING - 2 and c == 0 and (more or g < GROUPS - 1):
                            act.wait_ge(k_split, u + 2)
                        act.activation(attn[:, i % RING, c * CH:(c + 1) * CH], ps[:, c, :],
                                       ACT.Exp).then_inc(st_exp, 1)

            def post(b, more):
                take_output(b, GROUPS - 1)
                act.preload_act_table(ACT.Gelu)

                def take_z(c):
                    act.wait_ge(z_tp, b * NC + c + 1)
                    act.copy(z_s[0:KRON, :], ps[0:KRON, 0, :]).then_inc(zh_ok, 1)
                    act.copy(z_s[2 * KRON:3 * KRON, :], ps[0:KRON, 0, :]).then_inc(zh_ok, 1)

                def hidden(c):
                    bc = b * NC + c
                    for f in range(FB):
                        act.wait_ge(h_mm, bc * FB + f + 1)
                        if f >= 2 * HG:
                            act.wait_ge(p_mm, bc * KC + f // 4 - 1)
                        act.activation(attn[:, f % (2 * HG), 0:CH], ps[:, f % 3, :], ACT.Gelu).then_inc(h_ok, 1)

                def take_mlp(c):
                    act.wait_ge(p_mm, (b * NC + c + 1) * KC)
                    act.copy(mlp_part[:, :], ps[:, 3, :]).then_inc(p_ev, 1)

                take_z(0)
                hidden(0)
                take_z(1)
                take_mlp(0)
                hidden(1)
                take_mlp(1)
                act.preload_act_table_set("natural_log_exp_and_others")

            run(act, side, scores, products, post)

        @block.tensor
        def _(pe):
            pe.wait_ge(ident_ok, 1)
            pe.wait_ge(const_ok, 2)
            pe.wait_ge(qkv_in, 16 * 2)

            pe.sem_inc(st_mm, 1)
            pe.sem_inc(gg_mm, 1)

            def side(b, g, more, n, what, part, u, step, steps):
                bank = side_bank(b, g, n)
                psb = ps[:, 6 + bank, :]
                if step == 0 and not (b is None and n < 2):
                    pe.wait_ge(side_free[bank], side_count(b, g, n))
                gn = 0 if b is None else (g + 1) % GROUPS
                if what == "x":
                    pe.wait_ge(xn_ok, (part + 1) if b is None else (b + 1) * TT + part + 1)
                    tile = (x_in, x_late)[part // 4][:, part % 4, :]
                    for k in range(KC):
                        mm = pe.transpose(psb[:, k * P:(k + 1) * P], tile[:, k * P:(k + 1) * P], ident[:, :])
                elif what in ("q", "k"):
                    if what == "q" and part == 0 and gn == 0 and step == 0:
                        for t in (TT - 2, TT - 1):
                            wait_side(pe, side_free, b, g, more, "x", t)
                    col = (what == "k") * DIM + gn * P
                    for k in range(KC * step // steps, KC * (step + 1) // steps):
                        mm = pe.matmul(psb, wqkv[:, k, col:col + P], xn_t[:, k, part * CH:(part + 1) * CH],
                                       start=(k == 0), stop=(k == KC - 1))
                elif what == "v":
                    for i in range(4 * step // steps, 4 * (step + 1) // steps):
                        t = 4 * part + i
                        for k in range(KC):
                            mm = pe.matmul(psb[:, i * P:(i + 1) * P], xn_t[:, k, t * P:(t + 1) * P],
                                           wqkv[:, k, 2 * DIM + g * P:2 * DIM + (g + 1) * P],
                                           start=(k == 0), stop=(k == KC - 1))
                elif what == "logit":
                    w = HG * GP_NUM
                    if part == 0:
                        for half in range(2):
                            wait_side(pe, side_free, b, g, more, "q", half)
                    for i in range(4):
                        t = 4 * part + i
                        mm = pe.matmul(psb[:, i * w:(i + 1) * w], src[:, t * P:(t + 1) * P], gpb[:, gn, :],
                                       start=True, stop=True)
                elif what == "g":
                    if part == 0:
                        pe.wait_ge(g_ok, u)
                    for i in range(4):
                        t = 4 * part + i
                        mm = pe.transpose(psb[:, i * P:(i + 1) * P],
                                          gw[:, HG * t:HG * (t + 1), :].rearrange("p h m -> p (h m)"), ident[:, :])
                elif what == "lse":
                    pe.wait_ge(lse_ok, (u - 1) * HG + part + 1)
                    mm = pe.transpose(psb[0:TT, 0:P], neg_lse[:, TT * part:TT * (part + 1)], ident[:, :])
                if step == steps - 1:
                    mm.then_inc(side_mm[bank], 1)

            def side_steps(b, g, more, i, u):
                for n, (at, what, part, length) in enumerate(side_work(g, more)):
                    if at <= i < at + length:
                        side(b, g, more, n, what, part, u + 1, i - at, length)

            def weigh_values(b, g, more, m, p):
                if m == 0 and p == 0:
                    for n in (len(side_work(g, more)) - 2, len(side_work(g, more)) - 1):
                        pe.wait_ge(side_free[side_bank(b, g, n)], side_count(b, g, n) + 1)
                if p == 0:
                    pe.wait_ge(vc_ok, (b * GROUPS + g) * TT + m + 2)
                for h in range(HG):
                    mm = pe.matmul(wide(3)[HEAD_DIM * h:HEAD_DIM * (h + 1), p * PW:(p + 1) * PW], vc[:, m % 2, h, :],
                                   attn[:, (HG * m + h) % RING, p * PW:(p + 1) * PW],
                                   start=(m == 0 and p % 2 == 0), stop=(m == TT - 1 and p % 2 == 1))
                mm.then_inc(av_mm, 1)

            def scores(b, g, more):
                u = b * GROUPS + g
                for i in range(NT):
                    h, t = i // TT, i % TT
                    if t == 0:
                        pe.wait_ge(stacked[h], (u + 1) * 6 * 16)
                    if i >= 3:
                        pe.wait_ge(s_exp, u * NT + i - 2)
                    elif g > 0 and i == 0:
                        pe.wait_ge(st_exp, u * NT * NC)
                    elif g > 0:
                        pe.wait_ge(a_ok, u * NT + i - 2)
                    for c in range(NC):
                        mm = pe.matmul(ps[:, 2 * (i % 3) + c, :], q_st[0:SPLIT, h, t * P:(t + 1) * P],
                                       k_st[0:SPLIT, h, c * CH:(c + 1) * CH], start=True, stop=True)
                    mm.then_inc(s_mm, 1)
                    if i == 1:
                        if g > 0:
                            for p in range(PIECES):
                                weigh_values(b, g - 1, True, TT - 1, p)
                        else:
                            pe.wait_ge(out_ok, b * TT + 1)
                    if i == 2:
                        pe.wait_ge(av_ev, u + 1)
                    side_steps(b, g, more, i, u)
                side_steps(b, g, more, NT, u)

            def products(b, g, more):
                u = b * GROUPS + g
                pe.wait_ge(s_exp, (u + 1) * NT)
                pe.wait_ge(g_stacked, (u + 1) * 6 * HG * 16)

                def transposed(n):
                    i, c = n // NC, n % NC
                    m, h = i // HG, i % HG
                    if m == 0 and c == 0:
                        pe.wait_ge(lse_in[h], (u + 1) * 32)
                    if i >= 1:
                        pe.wait_ge(st_exp, u * NT * NC + n - 1)
                    pe.matmul(ps[:, c, :], k_st[:, h, m * P:(m + 1) * P], q_st[:, h, c * CH:(c + 1) * CH],
                              start=True, stop=True).then_inc(st_mm, 1)

                def group_weights(i):
                    m, h = i // HG, i % HG
                    if i >= 2:
                        pe.wait_ge(a_ok, u * NT + i - 1)
                    for c in range(NC):
                        mm = pe.matmul(ps[:, 2 + NC * (i % 2) + c, :], ga_st[:, h, m * P:(m + 1) * P],
                                       gb_st[:, h, c * CH:(c + 1) * CH], start=True, stop=True)
                    mm.then_inc(gg_mm, 1)

                transposed(0)
                transposed(1)
                ahead = 2
                for i in range(NT):
                    group_weights(i)
                    target = NC * min(i + (2 if i < 2 else 3 if i < 4 else 4), NT)
                    n = i - HG - 2
                    behind = n >= 0 and n % PIECES == 0
                    while ahead < target - (0 if behind else 1):
                        transposed(ahead)
                        ahead += 1
                    if n >= 0:
                        weigh_values(b, g, more, n // PIECES, n % PIECES)
                    while ahead < target:
                        transposed(ahead)
                        ahead += 1
                for n in range(NT - HG - 2, NT - HG):
                    weigh_values(b, g, more, n // PIECES, n % PIECES)

            def post(b, more):
                def project(c):
                    for i in range(4):
                        t = 4 * c + i
                        for k in range(KC):
                            mm = pe.matmul(ps[:, 4 * c + i, 0:DIM], attn_t[:, k, t * P:(t + 1) * P], wproj[:, k, :],
                                           start=(k == 0), stop=(k == KC - 1))
                        mm.then_inc(pj_mm, 1)

                def transpose_z(c):
                    pe.wait_ge(z_ok, b * NC + c + 1)
                    for i in range(4):
                        mm = pe.transpose(ps[0:KRON, 0, i * P:(i + 1) * P], z[:, i, :], ident[:, :])
                    mm.then_inc(z_tp, 1)

                def mlp(c):
                    bc = b * NC + c
                    pe.wait_ge(zh_ok, 2 * (bc + 1))
                    pe.wait_ge(zl_ok, 2 * (bc + 1))

                    def mlp_out(r):
                        pe.wait_ge(h_ok, bc * FB + 4 * r + 4)
                        for j in range(4):
                            f = 4 * r + j
                            mm = pe.matmul(ps[KRON * j:KRON * (j + 1), 3, :], p1_s[:, f, :],
                                           attn[:, f % (2 * HG), 0:CH], start=(r == 0), stop=(r == FB // 4 - 1))
                        mm.then_inc(p_mm, 1)

                    for f in range(FB):
                        if f >= 3:
                            pe.wait_ge(h_ok, bc * FB + f - 2)
                        pe.matmul(ps[:, f % 3, :], fc1_s[:, f * P:(f + 1) * P], z_s[:, :],
                                  start=True, stop=True).then_inc(h_mm, 1)
                        if f % 4 == 2 and f > 4:
                            mlp_out(f // 4 - 1)
                    if c == 0:
                        pe.wait_ge(h_ok, bc * FB + FB - 2)
                        transpose_z(1)
                    mlp_out(FB // 4 - 1)

                def spread(c):
                    pe.wait_ge(p_ev, b * NC + c + 1)
                    for i in range(4):
                        pe.matmul(ps[:, 4 + i, 0:DIM], mlp_part[:, i * P:(i + 1) * P], p2_s[:, :],
                                  start=True, stop=True).then_inc(e_mm, 1)

                for p in range(PIECES):
                    weigh_values(b, GROUPS - 1, more, TT - 1, p)
                pe.wait_ge(av_ev, (b + 1) * GROUPS + 1)
                project(0)
                project(1)
                transpose_z(0)
                mlp(0)
                pe.wait_ge(y_ok, b * TT + 8)
                spread(0)
                mlp(1)
                pe.wait_ge(out_ok, b * TT + 5)
                spread(1)

            for n, (_, what, part, _) in enumerate(FIRST):
                side(None, 0, True, n, what, part, 0, 0, 1)
            pe.wait_ge(weights_in, 16 * 5)
            pe.wait_ge(fc1_ok, 2)
            run(pe, lambda *a: None, scores, products, post)

        @block.vector
        def _(dve):
            dve.memset(k_st[SPLIT:AUG, :, :].bitcast(F32), 1.0).then_inc(const_ok, 1)
            dve.sem_inc(out_ok, 1)
            dve.wait_ge(t_in, 16)
            dve.tensor_scalar(tpar[:, 7:8], tpar[:, 0:1], -1.0, None, ALU.mult).then_inc(t_neg, 1)
            dve.wait_ge(t_neg, 1)
            dve.tensor_tensor(tpar[:, 1:2], tpar[:, 0:1], tpar[:, 7:8], ALU.min).then_inc(t_dve, 1)
            dve.wait_ge(t_act, 1)
            dve.scalar_tensor_tensor(tpar[:, 4:5], tpar[:, 0:1], 0.0, tpar[:, 3:4], ALU.max, ALU.add).then_inc(t_dve, 1)
            dve.wait_ge(t_dve, 2)
            dve.tensor_scalar(tpar[:, 5:6], tpar[:, 4:5], SCALE, None, ALU.mult).then_inc(t_dve, 1)
            dve.wait_ge(t_dve, 3)
            dve.reciprocal(tpar[:, 6:7], tpar[:, 5:6]).then_inc(t_dve, 1)

            steps = {"first": TT + 3, "batch": TT + GROUPS * 3 + NC * 9, "base": 0, "n": 0}

            def mark(ins):
                steps["n"] += 1
                ins.then_inc(dve_step, 1)

            def settle():
                dve.wait_ge(dve_step, steps["base"] + steps["n"])

            def step(ins):
                mark(ins)
                settle()

            def x_tile(t):
                return (x_in, x_late)[t // 4][:, t % 4, :]

            def x_stats(b, t):
                if t % 4 == 0:
                    dve.wait_ge(x_loaded[t // 4], 16 * (b + 1))
                step(dve.bn_stats(x_stats_s[:, t, 0:6], x_tile(t)))
                stand_alone(dve, "dve")
                dve.bn_aggr(x_stats_s[:, t, 6:8], x_stats_s[:, t, 0:6]).then_inc(x_stat, 1)

            def norm_x(b, t):
                dve.wait_ge(x_rstd_ok, b * TT + t + 1)
                dve.tensor_scalar(x_tile(t), x_tile(t), x_stats_s[:, t, 6:7], x_rstd[:, t:t + 1],
                                  ALU.subtract, ALU.mult).then_inc(xn_ok, 1)

            def side(b, g, more, n, what, part, u):
                bank = side_bank(b, g, n)
                psb = ps[:, 6 + bank, :]
                if what == "x":
                    if b is None:
                        x_stats(0, part)
                        norm_x(0, part)
                elif what == "logit":
                    dve.wait_ge(side_mm[bank], side_count(b, g, n) + 1)
                    w = NT // 2
                    logits = psb[:, 0:w * GP_NUM].rearrange("p (a m) -> p a m", m=GP_NUM)
                    step(dve.tensor_reduce(gmax[:, w * part:w * (part + 1)], logits, X, ALU.max))
                    dve.tensor_tensor(gw[:, w * part:w * (part + 1), 0:GP_NUM], logits,
                                      gmax[:, w * part:w * (part + 1)].unsqueeze(2).broadcast_to([P, w, GP_NUM]),
                                      ALU.subtract).then_inc(side_free[bank], 1)
                elif what == "k" and part == 0:
                    dve.wait_ge(g_exp, u + 1)
                    step(dve.tensor_reduce(gsum[:, :], gw[:, :, 0:GP_NUM], X, ALU.add))
                    dve.reciprocal(grec[:, :], gsum[:, :]).then_inc(g_rec, 1)
                elif what == "lse":
                    dve.wait_ge(side_mm[bank], side_count(b, g, n) + 1)
                    if part > 0:
                        dve.wait_ge(lse_in[part - 1], u * 32)
                    dve.tensor_copy(lse_hi[:, :], psb[0:TT, 0:P]).then_inc(lse_hi_ok, 1)
                    dve.wait_ge(lse_hi_ok, (u - 1) * HG + part + 1)
                    dve.tensor_tensor(lse_lo[:, :], psb[0:TT, 0:P], lse_hi[:, :].bitcast(F32),
                                      ALU.subtract).then_inc(side_free[bank], 1)

            def scores(b, g, more):
                u = b * GROUPS + g

                def lse(h):
                    cols = slice(TT * h, TT * (h + 1))
                    dve.wait_ge(s_log, u * HG + h + 1)
                    dve.tensor_tensor(neg_lse[:, cols], neg_max[:, cols], log_sum[:, cols],
                                      ALU.subtract).then_inc(lse_ok, 1)

                for i in range(NT):
                    dve.wait_ge(s_mm, u * NT + i + 1)
                    dve.tensor_reduce(neg_max[:, i:i + 1], wide(i % 3), X, ALU.max, negate=True).then_inc(s_max, 1)
                    if i % TT == 2 and i > TT:
                        lse(i // TT - 1)
                    if g == GROUPS - 1 and more:
                        if 6 <= i <= 9:
                            x_stats(b + 1, i - 2)
                        if 8 <= i <= 11:
                            norm_x(b + 1, i - 4)
                    between(lambda what: 2 if what == "k" else 0, i, side, b, g, more, u)
                lse(HG - 1)
                between(lambda what: 0, NT, side, b, g, more, u)

            def products(b, g, more):
                u = b * GROUPS + g
                def inverse_sums(m):
                    dve.wait_ge(a_ok, u * NT + HG * (m + 1))
                    if m >= 2:
                        dve.wait_ge(vc_ok, u * TT + m)
                    dve.reciprocal(crec[:, m % 2, :], csum[:, m % 2, :]).then_inc(c_ok, 1)

                for i in range(NT):
                    m, h = i // HG, i % HG
                    dve.wait_ge(st_exp, (u * NT + i + 1) * NC)
                    dve.wait_ge(gg_mm, u * NT + i + 2)
                    a = attn[:, i % RING, :]
                    dve.tensor_tensor_reduce(a, wide(1 + i % 2), a, 1.0, 1e-8, ALU.mult, ALU.add,
                                             csum[:, m % 2, h:h + 1]).then_inc(a_ok, 1)
                    if m > 0 and h == 0:
                        inverse_sums(m - 1)
                    if g == GROUPS - 2 and more and h == 2:
                        if 1 <= m <= 4:
                            x_stats(b + 1, m - 1)
                        if 2 <= m <= 5:
                            norm_x(b + 1, m - 2)
                inverse_sums(TT - 1)

            def post(b, more):
                def residual(c):
                    bc = b * NC + c
                    yt = (y, x_in)[c]
                    dve.wait_ge(y_in[c], 16 * (b + 1))
                    for i in range(4):
                        dve.wait_ge(pj_mm, bc * 4 + i + 1)
                        dve.tensor_tensor(yt[:, i, :], ps[:, 4 * c + i, 0:DIM], yt[:, i, :], ALU.add).then_inc(y_ok, 1)
                    for i in range(4):
                        dve.wait_ge(y_ok, bc * 4 + i + 1)
                        mark(dve.bn_stats(y_stats_s[:, i, 0:6], yt[:, i, :]))
                    settle()
                    stand_alone(dve, "dve")
                    for i in range(4):
                        dve.bn_aggr(y_stats_s[:, i, 6:8], y_stats_s[:, i, 0:6]).then_inc(y_stat, 1)
                    dve.wait_ge(y_stat, bc * 4 + 4)
                    for i in range(4):
                        mark(dve.scalar_tensor_tensor(yn[:, i, :], yt[:, i, :], y_stats_s[:, i, 6:7], fc2_row[:, :],
                                                      ALU.subtract, ALU.mult))
                    settle()
                    step(dve.tensor_reduce(z[:, :, :], yn[:, :, :].rearrange("p i (j l) -> p i j l", l=KIN),
                                           X, ALU.add))
                    dve.wait_ge(y_rstd_ok, bc + 1)
                    dve.tensor_tensor(z[:, :, :], z[:, :, :], y_rstd[:, :].unsqueeze(2).broadcast_to([P, 4, KRON]),
                                      ALU.mult).then_inc(z_ok, 1)

                def split_z(c):
                    bc = b * NC + c
                    dve.wait_ge(zh_ok, 2 * (bc + 1))
                    for r in (1, 3):
                        dve.tensor_tensor(z_s[KRON * r:KRON * (r + 1), :], ps[0:KRON, 0, :],
                                          z_s[0:KRON, :].bitcast(F32), ALU.subtract).then_inc(zl_ok, 1)

                def output(c):
                    yt = (y, x_in)[c]
                    for i in range(4):
                        dve.wait_ge(e_mm, b * TT + 4 * c + i + 1)
                        dve.tensor_tensor(yt[:, i, :], ps[:, 4 + i, 0:DIM], yt[:, i, :], ALU.add).then_inc(out_ok, 1)

                residual(0)
                split_z(0)
                residual(1)
                split_z(1)
                output(0)
                output(1)

            for n, (_, what, part, _) in enumerate(FIRST):
                side(None, 0, True, n, what, part, 0)
            assert steps["n"] == steps["first"], steps

            def batch(b, more):
                steps["base"], steps["n"] = steps["first"] + b * steps["batch"], 0
                for g in range(GROUPS):
                    scores(b, g, more)
                    products(b, g, more)
                post(b, more)

            with dve.Fori(0, BATCH - 1) as b:
                batch(b, True)
                assert steps["n"] == steps["batch"], steps
            batch(BATCH - 1, False)


def kernel(x, L0_conv_W_qkv, L0_conv_gp_w, L0_conv_t_param, L0_conv_W_proj,
           L0_ffn_c_fc_1, L0_ffn_c_fc_2, L0_ffn_c_proj_1, L0_ffn_c_proj_2):
    import numpy as np
    import concourse.bacc as bacc
    from concourse.bass_utils import run_bass_kernel_spmd

    def rows(w):
        w = np.asarray(w)
        return np.ascontiguousarray(w.reshape(-1, P, w.shape[1]).transpose(1, 0, 2))

    gp = np.asarray(L0_conv_gp_w).reshape(GROUPS, HG, GP_NUM, HEAD_DIM)
    blocks = np.zeros((HG, HEAD_DIM, GROUPS, HG, GP_NUM), gp.dtype)
    for j in range(HG):
        blocks[j, :, :, j, :] = gp[:, j].transpose(2, 0, 1)
    spread = np.zeros((4, KRON, KRON, KIN), np.asarray(L0_ffn_c_proj_2).dtype)
    for j in range(KRON):
        spread[:, j, j, :] = np.asarray(L0_ffn_c_proj_2)[:, 0]
    arrays = {
        "x": np.ascontiguousarray(np.asarray(x).reshape(BATCH, TOK, DIM)),
        "w_qkv": rows(L0_conv_W_qkv),
        "w_proj": rows(L0_conv_W_proj),
        "gp_blocks": blocks.reshape(P, GROUPS, HG * GP_NUM),
        "t_param": np.ascontiguousarray(np.broadcast_to(np.asarray(L0_conv_t_param).reshape(1, 1), (P, 1))),
        "fc1": np.ascontiguousarray(np.tile(np.asarray(L0_ffn_c_fc_1).T, (4, 1))),
        "fc2": np.ascontiguousarray(np.broadcast_to(np.tile(np.asarray(L0_ffn_c_fc_2)[0], KRON), (P, DIM))),
        "p1": np.ascontiguousarray(np.asarray(L0_ffn_c_proj_1).reshape(KRON, FB, P).transpose(2, 1, 0)),
        "p2": spread.reshape(P, DIM),
    }
    nc = bacc.Bacc("TRN2", target_bir_lowering=False, num_devices=1)
    args = [nc.dram_tensor(name, a.shape, mybir.dt.from_np(a.dtype), kind="ExternalInput").ap()
            for name, a in arrays.items()]
    args.append(nc.dram_tensor("out", (BATCH, TOK, DIM), F32, kind="ExternalOutput").ap())
    metaformer_layer(nc, *args)
    r = run_bass_kernel_spmd(nc, [arrays], core_ids=[0])
    return r.results[0]["out"].reshape(np.asarray(x).shape)
```
